# Optimizing a Trainium2 kernel written in Bass

```python
import numpy as np
import jax
import jax.numpy as jnp

def _softmax(x, axis=-1):
    return jax.nn.softmax(x, axis=axis)

def _gelu(x):
    return jax.nn.gelu(x, approximate=True)

def _silu(x):
    return jax.nn.silu(x)

def _sigmoid(x):
    return jax.nn.sigmoid(x)

def _layernorm(x, axis=-1, eps=1e-05):
    m = jnp.mean(x, axis=axis, keepdims=True)
    v = jnp.var(x, axis=axis, keepdims=True)
    return (x - m) / jnp.sqrt(v + eps)

def _scatter_add(tgt, idx, src, axis=0):
    return tgt.at[idx].add(src)

def _segment_sum(src, seg, n):
    return jax.ops.segment_sum(src, seg, n)
kernel_name = 'mk_decoder_preln_d1_seqx_r4_cf7336'

def setup_inputs(seed: int=0):
    np.random.seed(seed)
    _w = jnp.asarray

    def _rec_inputs():
        import jax
        import jax.numpy as jnp
        _rk = jax.random.key(seed)
        x = 7.22e-05 + 1 * jax.random.normal(jax.random.fold_in(_rk, 1), (8, 112, 256), jnp.float32)
        _lenS = 112 - jax.random.randint(jax.random.fold_in(_rk, 7), (8,), 0, max(1, 112 // 4) + 1, jnp.int32)
        _lenS2 = 375 - jax.random.randint(jax.random.fold_in(_rk, 8), (8,), 0, max(1, 375 // 4) + 1, jnp.int32)
        _ctx_1024P = jax.random.normal(jax.random.fold_in(_rk, 11), (8, 16, 256), jnp.float32)
        _ctx_1024c = jax.random.dirichlet(jax.random.fold_in(_rk, 511), 0.3 * jnp.ones((16,), jnp.float32), (8, 375))
        _ctx_1024t = jnp.einsum('bsk,bkd->bsd', _ctx_1024c, _ctx_1024P)
        _ctx_1024t = _ctx_1024t * jax.lax.rsqrt(jnp.mean(jnp.square(_ctx_1024t)) + 1e-12) * 0.953939
        ctx_1024 = 4.13588e-05 + 0.999923 * (_ctx_1024t + 0.3 * jax.random.normal(jax.random.fold_in(_rk, 611), (8, 375, 256), jnp.float32))
        _validS = jnp.arange(112)[None, :] < _lenS[:, None]
        _validS2 = jnp.arange(375)[None, :] < _lenS2[:, None]
        _causal = jnp.tril(jnp.ones((112, 112), dtype=bool))
        mask_Bx1xSxS2_ik1 = jnp.where(jnp.broadcast_to(_validS2[:, None, None, :], (8, 1, 112, 375)), 1, 0).astype(jnp.int32)
        return (x, ctx_1024, mask_Bx1xSxS2_ik1)
    x, ctx_1024, mask_Bx1xSxS2_ik1 = _rec_inputs()

    def _L0_attn_setup():
        import jax, jax.numpy as jnp
        import numpy as np
        EMBED, HID, H = (256, 256, 16)
        D = HID // H
        B, L = (4, 1024)

        def _layernorm(x, g, b, eps=1e-05):
            mu = jnp.mean(x, axis=-1, keepdims=True)
            var = jnp.mean(jnp.square(x - mu), axis=-1, keepdims=True)
            return (x - mu) * jax.lax.rsqrt(var + eps) * g + b

        def _affine_combine(x, y):
            a1, b1 = x
            a2, b2 = y
            return (a1 * a2, a2 * b1 + b2)
        key = jax.random.key(seed)
        ks = jax.random.split(key, 16)
        s = 0.02
        return {'emb': jax.random.normal(ks[0], (B, L, EMBED), jnp.float32), 'Wa_w': jax.random.normal(ks[1], (HID, EMBED), jnp.float32) * s, 'Wa_b': jnp.zeros((HID,), jnp.float32), 'Wb_w': jax.random.normal(ks[2], (HID, EMBED), jnp.float32) * s, 'Wb_b': jnp.zeros((HID,), jnp.float32), 'Wo_w': jax.random.normal(ks[3], (HID, EMBED), jnp.float32) * s, 'Wo_b': jnp.zeros((HID,), jnp.float32), 'C_w': jax.random.normal(ks[4], (HID, HID), jnp.float32) * s, 'C_b': jnp.zeros((HID,), jnp.float32), 'ln_g': jnp.ones((HID,), jnp.float32), 'ln_b': jnp.zeros((HID,), jnp.float32), 'f1_w': jax.random.normal(ks[5], (4 * HID, HID), jnp.float32) * s, 'f1_b': jnp.zeros((4 * HID,), jnp.float32), 'f2_w': jax.random.normal(ks[6], (HID, 4 * HID), jnp.float32) * s, 'f2_b': jnp.zeros((HID,), jnp.float32), 'p_w': jax.random.normal(ks[7], (HID, HID), jnp.float32) * s, 'p_b': jnp.zeros((HID,), jnp.float32), 'head_weights': jnp.ones((H,), jnp.float32)}
    _L0_attn_all = _L0_attn_setup()
    _L0_attn_in = {k: v for k, v in _L0_attn_all.items() if k in ('Wa_w', 'Wa_b', 'Wb_w', 'Wb_b', 'Wo_w', 'Wo_b', 'C_w', 'C_b', 'ln_g', 'ln_b', 'f1_w', 'f1_b', 'f2_w', 'f2_b', 'p_w', 'p_b', 'head_weights')}
    del _L0_attn_all

    def _L0_xattn_setup():
        import jax, jax.numpy as jnp
        import numpy as np
        D_MODEL = 256
        N_HEADS = 16
        D_K = D_MODEL // N_HEADS

        def _head_split(x):
            B, S, D = x.shape
            return x.reshape(B, S, N_HEADS, D_K).transpose(0, 2, 1, 3)
        key = jax.random.key(seed)
        ks = jax.random.split(key, 11)
        B, S, D = (4, 512, D_MODEL)
        inp = {'q': jax.random.normal(ks[0], (B, S, D), jnp.float32), 'k': jax.random.normal(ks[1], (B, S, D), jnp.float32), 'v': jax.random.normal(ks[2], (B, S, D), jnp.float32), 'mask': jax.random.randint(ks[3], (B, 1, S, S), 0, 2, jnp.int32), 'Wq': jax.random.normal(ks[4], (D, D), jnp.float32) / np.sqrt(D), 'bq': jax.random.normal(ks[5], (D,), jnp.float32) / np.sqrt(D), 'Wk': jax.random.normal(ks[6], (D, D), jnp.float32) / np.sqrt(D), 'bk': jax.random.normal(ks[7], (D,), jnp.float32) / np.sqrt(D), 'Wv': jax.random.normal(ks[8], (D, D), jnp.float32) / np.sqrt(D), 'bv': jax.random.normal(ks[9], (D,), jnp.float32) / np.sqrt(D)}
        return inp
    _L0_xattn_all = _L0_xattn_setup()
    _L0_xattn_in = {k: v for k, v in _L0_xattn_all.items() if k in ('Wq', 'bq', 'Wk', 'bk', 'Wv', 'bv')}
    del _L0_xattn_all

    def _L0_ffn_setup():
        import jax, jax.numpy as jnp
        import numpy as np
        B, S, H = (2, 256, 256)
        E, F = (8, 1024)
        GATE_TEMP = 0.1
        key = jax.random.key(seed)
        ks = jax.random.split(key, 6)
        s_h = 1.0 / np.sqrt(H)
        s_f = 1.0 / np.sqrt(F)
        return {'hidden_states': jax.random.normal(ks[0], (B, S, H), dtype=jnp.float32), 'w_router': jax.random.normal(ks[1], (H, E), dtype=jnp.float32) * s_h, 'w_gating': jax.random.normal(ks[2], (H, E), dtype=jnp.float32) * s_h, 'w_gate': jax.random.normal(ks[3], (E, H, F), dtype=jnp.float32) * s_h, 'w_up': jax.random.normal(ks[4], (E, H, F), dtype=jnp.float32) * s_h, 'w_down': jax.random.normal(ks[5], (E, F, H), dtype=jnp.float32) * s_f}
    _L0_ffn_all = _L0_ffn_setup()
    _L0_ffn_in = {k: v for k, v in _L0_ffn_all.items() if k in ('w_router', 'w_gating', 'w_gate', 'w_up', 'w_down')}
    del _L0_ffn_all
    return {'x': x, 'ctx_1024': ctx_1024, 'mask_Bx1xSxS2_ik1': mask_Bx1xSxS2_ik1, 'L0_attn_Wa_w': _L0_attn_in['Wa_w'], 'L0_attn_Wa_b': _L0_attn_in['Wa_b'], 'L0_attn_Wb_w': _L0_attn_in['Wb_w'], 'L0_attn_Wb_b': _L0_attn_in['Wb_b'], 'L0_attn_Wo_w': _L0_attn_in['Wo_w'], 'L0_attn_Wo_b': _L0_attn_in['Wo_b'], 'L0_attn_C_w': _L0_attn_in['C_w'], 'L0_attn_C_b': _L0_attn_in['C_b'], 'L0_attn_ln_g': _L0_attn_in['ln_g'], 'L0_attn_ln_b': _L0_attn_in['ln_b'], 'L0_attn_f1_w': _L0_attn_in['f1_w'], 'L0_attn_f1_b': _L0_attn_in['f1_b'], 'L0_attn_f2_w': _L0_attn_in['f2_w'], 'L0_attn_f2_b': _L0_attn_in['f2_b'], 'L0_attn_p_w': _L0_attn_in['p_w'], 'L0_attn_p_b': _L0_attn_in['p_b'], 'L0_attn_head_weights': _L0_attn_in['head_weights'], 'L0_xattn_Wq': _L0_xattn_in['Wq'], 'L0_xattn_bq': _L0_xattn_in['bq'], 'L0_xattn_Wk': _L0_xattn_in['Wk'], 'L0_xattn_bk': _L0_xattn_in['bk'], 'L0_xattn_Wv': _L0_xattn_in['Wv'], 'L0_xattn_bv': _L0_xattn_in['bv'], 'L0_ffn_w_router': _L0_ffn_in['w_router'], 'L0_ffn_w_gating': _L0_ffn_in['w_gating'], 'L0_ffn_w_gate': _L0_ffn_in['w_gate'], 'L0_ffn_w_up': _L0_ffn_in['w_up'], 'L0_ffn_w_down': _L0_ffn_in['w_down']}

def reference(x, ctx_1024, mask_Bx1xSxS2_ik1, L0_attn_Wa_w, L0_attn_Wa_b, L0_attn_Wb_w, L0_attn_Wb_b, L0_attn_Wo_w, L0_attn_Wo_b, L0_attn_C_w, L0_attn_C_b, L0_attn_ln_g, L0_attn_ln_b, L0_attn_f1_w, L0_attn_f1_b, L0_attn_f2_w, L0_attn_f2_b, L0_attn_p_w, L0_attn_p_b, L0_attn_head_weights, L0_xattn_Wq, L0_xattn_bq, L0_xattn_Wk, L0_xattn_bk, L0_xattn_Wv, L0_xattn_bv, L0_ffn_w_router, L0_ffn_w_gating, L0_ffn_w_gate, L0_ffn_w_up, L0_ffn_w_down):
    import jax
    import jax.numpy as jnp

    def _L0_attn_ref(emb, Wa_w, Wa_b, Wb_w, Wb_b, Wo_w, Wo_b, C_w, C_b, ln_g, ln_b, f1_w, f1_b, f2_w, f2_b, p_w, p_b, head_weights):
        import jax, jax.numpy as jnp
        import numpy as np
        EMBED, HID, H = (256, 256, 16)
        D = HID // H
        B, L = (4, 1024)

        def _layernorm(x, g, b, eps=1e-05):
            mu = jnp.mean(x, axis=-1, keepdims=True)
            var = jnp.mean(jnp.square(x - mu), axis=-1, keepdims=True)
            return (x - mu) * jax.lax.rsqrt(var + eps) * g + b

        def _affine_combine(x, y):
            a1, b1 = x
            a2, b2 = y
            return (a1 * a2, a2 * b1 + b2)
        Bv, Lv, _ = emb.shape
        a = jnp.tanh(emb @ Wa_w.T + Wa_b).reshape(Bv, Lv, H, D)
        b = (emb @ Wb_w.T + Wb_b).reshape(Bv, Lv, H, D)
        w = (emb @ Wo_w.T + Wo_b).reshape(Bv, Lv, H, D)
        _, h_seq = jax.lax.associative_scan(_affine_combine, (a, b), axis=1)
        c_out = (h_seq.reshape(Bv, Lv, HID) @ C_w.T + C_b).reshape(Bv, Lv, H, D)
        z = (head_weights[None, None, :, None] * (c_out + w)).reshape(Bv, Lv, HID)
        u = z + _layernorm(z, ln_g, ln_b)
        ffn = jax.nn.gelu(u @ f1_w.T + f1_b, approximate=False)
        out = ffn @ f2_w.T + f2_b
        return (u + out) @ p_w.T + p_b

    def _L0_xattn_ref(q, k, v, mask, Wq, bq, Wk, bk, Wv, bv):
        import jax, jax.numpy as jnp
        import numpy as np
        D_MODEL = 256
        N_HEADS = 16
        D_K = D_MODEL // N_HEADS

        def _head_split(x):
            B, S, D = x.shape
            return x.reshape(B, S, N_HEADS, D_K).transpose(0, 2, 1, 3)
        B, S, D = q.shape
        qh = _head_split(q @ Wq.T + bq)
        kh = _head_split(k @ Wk.T + bk)
        vh = _head_split(v @ Wv.T + bv)
        scores = jnp.einsum('bhqd,bhkd->bhqk', qh, kh) / np.sqrt(D_K).astype(np.float32)
        scores = jnp.where(mask == 0, -jnp.inf, scores)
        probs = jax.nn.softmax(scores, axis=-1)
        probs = jnp.where(jnp.isnan(probs), 0.0, probs)
        out = jnp.einsum('bhqk,bhkd->bhqd', probs, vh)
        return out.transpose(0, 2, 1, 3).reshape(B, S, D)

    def _L0_ffn_ref(hidden_states, w_router, w_gating, w_gate, w_up, w_down):
        import jax, jax.numpy as jnp
        import numpy as np
        B, S, H = (2, 256, 256)
        E, F = (8, 1024)
        GATE_TEMP = 0.1
        x = hidden_states
        router_probs = jax.nn.softmax(jnp.einsum('bsh,he->bse', x, w_router), axis=-1)
        gate_weights = jax.nn.softmax(jnp.einsum('bsh,he->bse', x, w_gating) / GATE_TEMP, axis=-1)
        g = jnp.einsum('bsh,ehf->ebsf', x, w_gate)
        u = jnp.einsum('bsh,ehf->ebsf', x, w_up)
        h = jax.nn.silu(g) * u
        expert_out = jnp.einsum('ebsf,efh->ebsh', h, w_down)
        cw = router_probs * gate_weights
        cw = cw / (jnp.sum(cw, axis=-1, keepdims=True) + 1e-09)
        out = jnp.einsum('ebsh,bse->bsh', expert_out, cw)
        return out
    x = x + _L0_attn_ref(_layernorm(x, axis=-1), L0_attn_Wa_w, L0_attn_Wa_b, L0_attn_Wb_w, L0_attn_Wb_b, L0_attn_Wo_w, L0_attn_Wo_b, L0_attn_C_w, L0_attn_C_b, L0_attn_ln_g, L0_attn_ln_b, L0_attn_f1_w, L0_attn_f1_b, L0_attn_f2_w, L0_attn_f2_b, L0_attn_p_w, L0_attn_p_b, L0_attn_head_weights)
    x = x + _L0_xattn_ref(_layernorm(x, axis=-1), ctx_1024, ctx_1024, mask_Bx1xSxS2_ik1, L0_xattn_Wq, L0_xattn_bq, L0_xattn_Wk, L0_xattn_bk, L0_xattn_Wv, L0_xattn_bv)
    x = x + _L0_ffn_ref(_layernorm(x, axis=-1), L0_ffn_w_router, L0_ffn_w_gating, L0_ffn_w_gate, L0_ffn_w_up, L0_ffn_w_down)
    return x

_drawn_inputs = setup_inputs


def setup_inputs(seed=0):
    import zlib

    import numpy as np

    out = dict(_drawn_inputs(seed))
    spreads = {'L0_attn_Wa_b': (0.0, 0.468),
     'L0_attn_Wb_b': (0.0, 0.1),
     'L0_attn_Wo_b': (0.0, 0.1),
     'L0_attn_C_b': (0.0, 0.1),
     'L0_attn_ln_g': (1.0, 0.2),
     'L0_attn_ln_b': (0.0, 0.1),
     'L0_attn_f1_b': (0.0, 0.593),
     'L0_attn_f2_b': (0.0, 0.1),
     'L0_attn_p_b': (0.0, 0.1),
     'L0_attn_head_weights': (1.0, 0.2)}
    factors = {'L0_xattn_bq': 3.315, 'L0_xattn_bk': 8.0}
    for name, (base, spread) in spreads.items():
        noise = np.random.default_rng([zlib.crc32(name.encode()), seed]).standard_normal(out[name].shape)
        drawn = base * np.exp(spread * noise) if base else spread * noise
        out[name] = jnp.asarray(drawn.astype(out[name].dtype))
    for name, factor in factors.items():
        out[name] = (out[name] * factor).astype(out[name].dtype)
    return out
```

```python
import concourse.bass as bass
from concourse import mybir
from contextlib import ExitStack

F32 = mybir.dt.float32
F32R = mybir.dt.float32r
I32 = mybir.dt.int32
ALU = mybir.AluOpType
ACT = mybir.ActivationFunctionType
AX = mybir.AxisListType

B, S, D = 8, 112, 256
SK = 375
H, DH = 16, 16
P = 128
KB = D // P
T = B * S
HALF = T // 2
BH = B // 2
FF = 1024
NF = FF // P
E = 8
KT, NK = 125, 3
HH = H // KB
HG = 4
VW = DH + 1
RING = 4
LEAD = RING - 1
LN_EPS = 1e-5
MASKED = -1e30
W_A, W_B, W_O, W_C, W_P, W_Q, W_K, W_V = range(8)
C_A, C_B, C_Q, C_K, C_F1, C_F2 = 0, 2, 4, 6, 8, 16
R_C, R_O, R_HEAD, R_G, R_B, R_P, R_V = range(7)
GATE_SCALE = 10.0 / (1.0 + 1.4901161193847656e-08)
TB = (0, 0, 2, 4, 4, 6, 0, 2)
ZB = (6, 0)


def decoder_layer(nc, x, context, mask, square, ff1, ff2, columns, rows, router, gate, up, down, constants, out):
    ctx = ExitStack()
    with ctx:
        def sb(name, shape, dt=F32, to=ctx):
            return to.enter_context(nc.sbuf_tensor(name, shape, dt))

        def sem(name):
            return ctx.enter_context(nc.semaphore(name))

        xs = sb("xs", [S, B, D])
        xpb = sb("xpb", [S, B, D])
        consts = sb("consts", [P, P + HH])
        cols = sb("cols", [P, 18])
        rowv = sb("rowv", [KT, 7, D])
        wsq = sb("wsq", [P, 8, KB, D])
        wrt = sb("wrt", [P, KB, 2 * E])
        stats = sb("stats", [S, 4, B, 6])
        mv = sb("mv", [S, 4, B, 2])
        var = sb("var", [S, 4, B])
        rstd = sb("rstd", [S, 4, B])
        nhalf = sb("nhalf", [S, B])
        raw = sb("raw", [P, 2, 12 * D])
        whi = sb("whi", [P, RING, 6 * P], F32R)
        wlo = sb("wlo", [P, RING, 6 * P], F32R)
        qhi = sb("qhi", [P, KB, T], F32R)
        qlo = sb("qlo", [P, KB, T], F32R)
        ident = consts[:, 0:P]
        headmask = consts[:, P:P + HH]
        cw_dram = nc.dram_tensor("cw_dram", (E, T), F32, kind="Internal").ap()
        bank = ctx.enter_context(nc.psum_tensor("bank", [P, 8, 512], F32))

        one = ctx.enter_context(ExitStack())
        xn = sb("xn", [S, B, D], to=one)
        zt = sb("zt", [S, B, D], to=one)
        nT = sb("nT", [P, KB, T], to=one)
        aT = sb("aT", [P, KB, T], to=one)
        bT = sb("bT", [P, KB, T], to=one)
        hT = sb("hT", [P, KB, T], to=one)
        bsum = sb("bsum", [S, D], to=one)
        uT, qf = aT, bT
        fT = sb("fT", [P, 2, T], to=one)
        fhi = sb("fhi", [P, 2, T], F32R, to=one)
        flo = sb("flo", [P, 2, T], F32R, to=one)
        w1hi = sb("w1hi", [P, 2, KB * FF // 2], F32R, to=one)
        w1lo = sb("w1lo", [P, 2, KB * FF // 2], F32R, to=one)
        w2hi = sb("w2hi", [P, 2, NF // 2 * D], F32R, to=one)
        w2lo = sb("w2lo", [P, 2, NF // 2 * D], F32R, to=one)
        uhi, ulo = qhi, qlo
        one.close()

        two = ctx.enter_context(ExitStack())
        cxt = sb("cxt", [P, 2, KB, SK], to=two)
        khi = sb("khi", [P, 2, KB, SK + 1], F32R, to=two)
        klo = sb("klo", [P, 2, KB, SK + 1], F32R, to=two)
        vs = sb("vs", [KT, 2, NK, H, VW], to=two)
        mask_in = sb("mask_in", [S, 2, SK], I32, to=two)
        mbias = sb("mbias", [S, 2, SK + 1], F32R, to=two)
        some = sb("some", [S, 2, 1], to=two)
        qbh = sb("qbh", [P, 2, KB, HH, S], F32R, to=two)
        qbl = sb("qbl", [P, 2, KB, HH, S], F32R, to=two)
        smax = sb("smax", [S, 2, H], to=two)
        scored = sb("scored", [S, 2, SK], to=two)
        diag = sb("diag", [S, KB, HH, S], F32R, to=two)
        irep = sb("irep", [S, HG, S], F32R, to=two)
        minus = sb("minus", [S, KT + 1], F32R, to=two)
        prob = sb("prob", [KT, KB, NK, HH * S], to=two)
        osum = sb("osum", [S, H], to=two)
        orec = sb("orec", [S, H], to=two)
        att = sb("att", [S, H, DH], to=two)
        two.close()

        three = ctx.enter_context(ExitStack())
        x3 = sb("x3", [S, B, D], to=three)
        x3T = sb("x3T", [P, KB, T], to=three)
        x3hi = sb("x3hi", [P, KB, T], F32R, to=three)
        x3lo = sb("x3lo", [P, KB, T], F32R, to=three)
        lg = sb("lg", [S, B, 2, E], to=three)
        lmax = sb("lmax", [S, B, 2], to=three)
        lsum = sb("lsum", [S, B, 2], to=three)
        cw = sb("cw", [S, B, E], to=three)
        cws = sb("cws", [S, B], to=three)
        cwT = sb("cwT", [E, T], to=three)
        cwb = sb("cwb", [P, E, T], to=three)
        sg = sb("sg", [P, 2, T], to=three)
        hid = sb("hid", [P, T], to=three)
        hhi = sb("hhi", [P, 2, T], F32R, to=three)
        hlo = sb("hlo", [P, 2, T], F32R, to=three)
        yw = sb("yw", [P, KB, T], to=three)
        acc = sb("acc", [P, KB, T], to=three)

        in_x = [sem(f"in_x{n}") for n in range(2)]
        in_consts, in_rows, in_ab, in_oc, in_pq, in_kv, in_router = map(
            sem, ("in_consts", "in_rows", "in_ab", "in_oc", "in_pq", "in_kv", "in_router"))
        in_ff = [sem(f"in_ff{n}") for n in range(2)]
        in_ctx = [sem(f"in_ctx{n}") for n in range(2)]
        in_mask = [sem(f"in_mask{n}") for n in range(2)]
        in_w = [sem(f"in_w{n}") for n in range(2)]
        out_cw, in_cw, out_done = sem("out_cw"), sem("in_cw"), sem("out_done")
        var_ready, rstd_ready, norm_ready = sem("var_ready"), sem("rstd_ready"), sem("norm_ready")
        dve_step = sem("dve_step")
        pool_step = sem("pool_step")
        turned, turned_out = sem("turned"), sem("turned_out")
        ab_done, a_ready, b_ready, h_ready = sem("ab_done"), sem("a_ready"), sem("b_ready"), sem("h_ready")
        z_done, u_ready = sem("z_done"), sem("u_ready")
        ffw_hi, ffw_lo, u_split = sem("ffw_hi"), sem("ffw_lo"), sem("u_split")
        f1_done, gelu_ready, f_split, f2_done, v_ready = (
            sem("f1_done"), sem("gelu_ready"), sem("f_split"), sem("f2_done"), sem("v_ready"))
        p_done, x1_ready, q_done, q_float, q_ready = (
            sem("p_done"), sem("x1_ready"), sem("q_done"), sem("q_float"), sem("q_ready"))
        kv_done, khi_ready, kv_out, mb_ready, mb_some = (
            sem("kv_done"), sem("khi_ready"), sem("kv_out"), sem("mb_ready"), sem("mb_some"))
        qb_ready, s_done, max_ready, diag_ready = (
            sem("qb_ready"), sem("s_done"), sem("max_ready"), sem("diag_ready"))
        st_done, exp_done, pv_done, o_out, o_step = (
            sem("st_done"), sem("exp_done"), sem("pv_done"), sem("o_out"), sem("o_step"))
        att_consts = sem("att_consts")
        passed = sem("passed")
        x3_float, x3_split, lg_done, soft_exp, lg_ready, cw_ready, cwT_done, cwT_ready = map(
            sem, ("x3_float", "x3_split", "lg_done", "soft_exp", "lg_ready", "cw_ready", "cwT_done", "cwT_ready"))
        w_hi, w_lo, g_done, u_done, silu_ready, h_float, hhi_ready, h_split = map(
            sem, ("w_hi", "w_lo", "g_done", "u_done", "silu_ready", "h_float", "hhi_ready", "h_split"))
        chunk_used, y_out, acc_done, fin_done, fin_out = map(
            sem, ("chunk_used", "y_out", "acc_done", "fin_done", "fin_out"))

        START = ((st_done, 1), (kv_out, 1), (max_ready, 2), (exp_done, 2), (pv_done, 2), (o_out, 1),
                 (diag_ready, 3), (chunk_used, RING), (silu_ready, 1), (h_float, 2), (h_split, 1),
                 (y_out, 1), (acc_done, 1))

        def started(s):
            return sum(n for other, n in START if other is s)

        def at(eng, s, count):
            eng.wait_ge(s, count + started(s))

        def at_all(eng, *counts):
            for s, n in counts:
                at(eng, s, n)
                eng.sem_inc(passed, 1)

        def begin(eng, *sems):
            for s in sems:
                eng.sem_inc(s, started(s))

        def half(b):
            return slice(b * HALF, (b + 1) * HALF)

        def seq(b):
            return slice(b * S, (b + 1) * S)

        def pair(n):
            return bank[:, n:n + 2, 0:HALF]

        gate_v = gate.rearrange("e (k p) f -> e p k f", p=P)
        up_v = up.rearrange("e (k p) f -> e p k f", p=P)
        down_v = down.rearrange("e (n p) d -> e p n d", p=P)

        def raw_part(slot, what):
            if what < 2:
                return raw[:, slot, what * 4 * D:(what + 1) * 4 * D].rearrange("p (k f) -> p k f", k=KB)
            return raw[:, slot, 8 * D:12 * D].rearrange("p (n d) -> p n d", n=4)

        def raw_chunk(slot, n, what):
            if what < 2:
                return raw_part(slot, what)[:, :, n * P:(n + 1) * P]
            return raw_part(slot, 2)[:, n, :]

        def chunk(w, r, what):
            part = w[:, r, what * 2 * P:(what + 1) * 2 * P]
            return part.rearrange("p (k f) -> p k f", k=KB) if what < 2 else part

        block = ctx.enter_context(nc.Block())

        @block.sync
        def _(sp):
            xv = x.rearrange("s (n b) d -> n s b d", n=2)
            sp.dma_start(xs[:, 0:BH, :], xv[0]).then_inc(in_x[0], 16)
            sp.dma_start(consts[:, :], constants).then_inc(in_consts, 16)
            sp.dma_start(cols[:, :], columns).then_inc(in_consts, 16)
            sp.dma_start(xs[:, BH:B, :], xv[1]).then_inc(in_x[1], 16)
            sp.dma_start(wsq[:, W_A:W_B + 1, :, :], square[:, W_A:W_B + 1, :, :]).then_inc(in_ab, 16)
            sp.dma_start(wsq[:, W_O:W_C + 1, :, :], square[:, W_O:W_C + 1, :, :]).then_inc(in_oc, 16)
            sp.dma_start(rowv[:, :, :], rows.rearrange("r d -> (r d)").partition_broadcast(KT)
                         .rearrange("s (r d) -> s r d", r=7)).then_inc(in_rows, 16)
            sp.dma_start(raw[:, 0, 0:KB * FF], ff1.rearrange("p k f -> p (k f)")).then_inc(in_ff[0], 16)
            sp.dma_start(raw[:, 1, 0:NF * D], ff2.rearrange("p n d -> p (n d)")).then_inc(in_ff[1], 16)
            sp.dma_start(wsq[:, W_P:W_Q + 1, :, :], square[:, W_P:W_Q + 1, :, :]).then_inc(in_pq, 16)
            sp.dma_start(wsq[:, W_K:W_V + 1, :, :], square[:, W_K:W_V + 1, :, :]).then_inc(in_kv, 16)
            sp.dma_start(wrt[:, :, :], router).then_inc(in_router, 16)

            def load_experts(e, s):
                f = slice(s * FF // 2, (s + 1) * FF // 2)
                n = slice(s * NF // 2, (s + 1) * NF // 2)
                sp.dma_start(raw_part(s, 0), gate_v[e, :, :, f]).then_inc(in_w[s], 16)
                sp.dma_start(raw_part(s, 1), up_v[e, :, :, f]).then_inc(in_w[s], 16)
                sp.dma_start(raw_part(s, 2), down_v[e, :, n, :]).then_inc(in_w[s], 16)

            def load_batch(b, s):
                sp.dma_start(cxt[:, s, :, :], context[b]).then_inc(in_ctx[s], 16)
                sp.dma_start(mask_in[:, s, :], mask[b]).then_inc(in_mask[s], 16)

            sp.wait_ge(ffw_hi, 4)
            sp.wait_ge(ffw_lo, 4)
            load_experts(0, 0)
            load_experts(0, 1)
            sp.wait_ge(q_ready, 2)
            load_batch(0, 0)
            load_batch(1, 1)
            with sp.Fori(0, 3) as i:
                for s in range(2):
                    at_all(sp, (kv_done, 5 * (2 * i + s) + 5), (mb_ready, 2 * i + s + 1))
                    load_batch(2 * i + 2 + s, s)
            with sp.Fori(1, E) as e:
                for s in range(2):
                    at_all(sp, (w_hi, 8 * (e - 1) + 4 * s + 4), (w_lo, 8 * (e - 1) + 4 * s + 4))
                    load_experts(e, s)
            ov = out.rearrange("b s d -> s b d")
            for n in range(4):
                sp.wait_ge(fin_out, n + 1)
                sp.dma_start(ov[:, 2 * n:2 * n + 2, :], xs[:, 2 * n:2 * n + 2, :]).then_inc(out_done, 16)
            sp.wait_ge(out_done, 64)

        @block.gpsimd
        def _(pool):
            count = [0]

            def link(ins):
                count[0] += 1
                ins.then_inc(pool_step, 1)
                pool.wait_ge(pool_step, count[0])

            begin(pool, diag_ready, acc_done)
            link(pool.memset(nhalf[:, :], -0.5))

            def rsqrt(ln, h):
                pool.wait_ge(var_ready, 2 * ln + h + 1)
                bs = slice(h * BH, (h + 1) * BH)
                pool.tensor_tensor(rstd[:, ln, bs], var[:, ln, bs], nhalf[:, bs], ALU.pow).then_inc(rstd_ready, 1)

            rsqrt(0, 0)
            rsqrt(0, 1)
            for n, (hi, lo) in enumerate(((w1hi, w1lo), (w2hi, w2lo))):
                for c in range(2):
                    pool.wait_ge(ffw_hi, 2 * n + c + 1)
                    src = raw[:, n, c * FF:(c + 1) * FF]
                    pool.tensor_tensor(lo[:, c, :], src, hi[:, c, :].bitcast(F32), ALU.subtract).then_inc(ffw_lo, 1)
            for ln in (1, 2):
                rsqrt(ln, 0)
                rsqrt(ln, 1)

            def spread(b, s):
                for k in range(KB):
                    for dst, src in ((qbh, qhi), (qbl, qlo)):
                        q = src[:, k, bass.ds(b * S, S)].bitcast(F32).unsqueeze(1).to_broadcast([P, HH, S])
                        m = headmask.unsqueeze(2).to_broadcast([P, HH, S])
                        pool.tensor_tensor(dst[:, s, k, :, :], q, m, ALU.mult).then_inc(qb_ready, 1)

            def diagonals(b, s, first=False):
                for k in range(KB):
                    at(pool, max_ready, H * b + HH * (k + 1))
                    if not first:
                        at(pool, st_done, 6 * (b - 1) + 3 * (k + 1))
                    i = ident[0:S, 0:S].unsqueeze(1).to_broadcast([S, HH, S])
                    m = smax[:, s, k * HH:(k + 1) * HH].unsqueeze(2).to_broadcast([S, HH, S])
                    pool.tensor_tensor(diag[:, k, :, :], i, m, ALU.mult).then_inc(diag_ready, 1)

            pool.wait_ge(q_ready, 2)
            spread(0, 0)
            diagonals(0, 0, True)

            def attend(b, s):
                at(pool, st_done, 6 * b)
                spread(b + 1, 1 - s)
                diagonals(b + 1, 1 - s)

            with pool.Fori(0, 3) as i:
                for s in range(2):
                    attend(2 * i + s, s)
            attend(6, 0)

            def split_low(e, n):
                at(pool, w_hi, 8 * e + n + 1)
                for what in range(3):
                    ins = pool.tensor_tensor(chunk(wlo, n % RING, what), raw_chunk(n // 4, n % 4, what),
                                             chunk(whi, n % RING, what).bitcast(F32), ALU.subtract)
                ins.then_inc(w_lo, 1)

            def accumulate(e):
                for m in range(KB):
                    at(pool, y_out, KB * e + m + 1)
                    at(pool, acc_done, KB * e + m)
                    pool.tensor_tensor(acc[:, m, :], acc[:, m, :], yw[:, m, :], ALU.add).then_inc(acc_done, 1)

            for n in range(LEAD):
                split_low(0, n)
            at(pool, o_out, B)
            link(pool.memset(acc[:, :, :], 0.0))
            rsqrt(3, 0)
            rsqrt(3, 1)
            for n in range(LEAD, NF):
                split_low(0, n)
            for n in range(LEAD):
                split_low(1, n)

            def expert(e, more):
                accumulate(e - 1)
                for n in range(LEAD, NF):
                    split_low(e, n)
                if more:
                    for n in range(LEAD):
                        split_low(e + 1, n)

            with pool.Fori(1, E - 1) as e:
                expert(e, True)
            expert(E - 1, False)
            accumulate(E - 1)

        @block.scalar
        def _(act):
            begin(act, exp_done, silu_ready)

            def turn_out(n, dst):
                act.wait_ge(turned, n + 1)
                act.activation(dst, pair(TB[n]), ACT.Copy).then_inc(turned_out, 1)

            turn_out(0, nT[:, :, half(0)])
            turn_out(1, nT[:, :, half(1)])
            act.wait_ge(in_consts, 32)
            for h in range(2):
                for m in range(KB):
                    act.wait_ge(ab_done, 4 * h + m + 1)
                    act.activation(aT[:, m, half(h)], bank[:, 2 + m, 0:HALF], ACT.Tanh,
                                   bias=cols[:, C_A + m:C_A + m + 1]).then_inc(a_ready, 1)
            for n, hi in enumerate((w1hi, w2hi)):
                act.wait_ge(in_ff[n], 16)
                for c in range(2):
                    act.activation(hi[:, c, :], raw[:, n, c * FF:(c + 1) * FF], ACT.Copy).then_inc(ffw_hi, 1)
            act.wait_ge(h_ready, 4)
            turn_out(2, uT[:, :, half(0)])
            turn_out(3, uT[:, :, half(1)])
            for n in range(NF):
                act.wait_ge(f1_done, n + 1)
                if n >= 2:
                    act.wait_ge(f_split, 2 * (n - 1))
                act.activation(fT[:, n % 2, :].rearrange("p (h t) -> p h t", h=2), pair(2 * (n % 2)), ACT.Gelu,
                               bias=cols[:, C_F1 + n:C_F1 + n + 1]).then_inc(gelu_ready, 1)
            turn_out(4, nT[:, :, half(0)])
            turn_out(5, nT[:, :, half(1)])

            def key_high(b, s, k):
                act.wait_ge(kv_done, 5 * b + k + 1)
                act.activation(khi[:, s, k, 0:SK], bank[:, 7, 0:SK], ACT.Identity,
                               bias=cols[:, C_K + k:C_K + k + 1]).then_inc(khi_ready, 1)

            def exps(b, u):
                k, t = u // NK, u % NK
                at(act, st_done, 6 * b + u + 1)
                at(act, pv_done, 2 * b + k - 1)
                act.activation(prob[:, k, t, :].rearrange("p (g t) -> p g t", g=2),
                               bank[0:KT, 2 + 2 * (u % 2):4 + 2 * (u % 2), 0:HG * S], ACT.Exp).then_inc(exp_done, 1)

            act.wait_ge(q_ready, 2)
            key_high(0, 0, 0)
            key_high(0, 0, 1)

            def attend(b, s, more):
                for u in range(6):
                    exps(b, u)
                    if more and u < 2:
                        key_high(b + 1, 1 - s, u)

            with act.Fori(0, 3) as i:
                for s in range(2):
                    attend(2 * i + s, s, True)
            attend(6, 0, True)
            attend(7, 1, False)

            def split_high(e, n):
                c = 8 * e + n
                if n % 4 == 0:
                    act.wait_ge(in_w[n // 4], 48 * (e + 1))
                at(act, chunk_used, c + 1 - RING)
                for what in range(3):
                    ins = act.activation(chunk(whi, n % RING, what), raw_chunk(n // 4, n % 4, what), ACT.Copy)
                ins.then_inc(w_hi, 1)

            for n in range(LEAD):
                split_high(0, n)
            turn_out(6, x3T[:, :, half(0)])
            turn_out(7, x3T[:, :, half(1)])
            act.wait_ge(lg_ready, 1)
            for j, scale in enumerate((1.0, GATE_SCALE)):
                act.activation(lg[:, :, j, :], lg[:, :, j, :], ACT.Exp, scale=scale).then_inc(soft_exp, 1)
            act.wait_ge(cwT_done, 1)
            act.activation(cwT[:, :].rearrange("e (h t) -> e h t", h=2), bank[0:E, 5:7, 0:HALF], ACT.Copy)\
               .then_inc(cwT_ready, 1)
            act.wait_ge(cwT_ready, 1)
            act.dma_start(cw_dram, cwT[:, :]).then_inc(out_cw, 16)
            act.wait_ge(out_cw, 16)
            act.dma_start(cwb[:, :, :].rearrange("p e t -> p (e t)"),
                          cw_dram.rearrange("e t -> (e t)").partition_broadcast(P)).then_inc(in_cw, 16)

            def silu(e, n):
                f = 8 * e + n
                act.wait_ge(g_done, f + 1)
                at(act, h_float, f - 1)
                act.activation(sg[:, n % 2, :].rearrange("p (h t) -> p h t", h=2), pair(0), ACT.Silu)\
                   .then_inc(silu_ready, 1)

            def expert(e, more):
                for n in range(NF):
                    silu(e, n)
                    if n < NF - LEAD:
                        split_high(e, n + LEAD)
                    elif more:
                        split_high(e + 1, n + LEAD - NF)

            with act.Fori(0, E - 1) as e:
                expert(e, True)
            expert(E - 1, False)

        @block.vector
        def _(dve):
            count = [0]

            def did(ins):
                count[0] += 1
                ins.then_inc(dve_step, 1)

            def sync():
                dve.wait_ge(dve_step, count[0])

            begin(dve, kv_out, max_ready, o_out, h_float, h_split, y_out)

            def statistics(ln, h, src):
                bs = range(h * BH, (h + 1) * BH)
                for b in bs:
                    did(dve.bn_stats(stats[:, ln, b, :], src[:, b, :]))
                sync()
                for b in bs:
                    did(dve.bn_aggr(mv[:, ln, b, :], stats[:, ln, b, :]))
                sync()
                dve.tensor_scalar(var[:, ln, bs.start:bs.stop], mv[:, ln, bs.start:bs.stop, 1], LN_EPS, None,
                                  ALU.add).then_inc(var_ready, 1)

            def normalize(ln, h, src, dst):
                dve.wait_ge(rstd_ready, 2 * ln + h + 1)
                for b in range(h * BH, (h + 1) * BH):
                    did(dve.tensor_scalar(dst[:, b, :], src[:, b, :], mv[:, ln, b, 0:1], rstd[:, ln, b:b + 1],
                                          ALU.subtract, ALU.mult))
                sync()

            for h in range(2):
                dve.wait_ge(in_x[h], 16)
                statistics(0, h, xs)
                normalize(0, h, xs, xn)
                dve.sem_inc(norm_ready, 1)
            dve.wait_ge(in_rows, 16)
            did(dve.tensor_tensor(bsum[:, :], rowv[0:S, R_C, :], rowv[0:S, R_O, :], ALU.add))
            did(dve.tensor_tensor(xpb[:, :, :], xs[:, :, :],
                                  rowv[0:S, R_P, :].unsqueeze(1).to_broadcast([S, B, D]), ALU.add))
            dve.wait_ge(in_consts, 32)
            for h in range(2):
                for m in range(KB):
                    dve.wait_ge(ab_done, 4 * h + 2 + m + 1)
                    dve.tensor_scalar(bT[:, m, half(h)], bank[:, 4 + m, 0:HALF], cols[:, C_B + m:C_B + m + 1], None,
                                      ALU.add).then_inc(b_ready, 1)
                for m in range(KB):
                    dve.wait_ge(a_ready, 2 * h + m + 1)
                    first = aT[:, m, half(h)].rearrange("p (b t) -> p b t", b=BH)[:, :, 0:1]
                    did(dve.memset(first, 0.0))
                    sync()
                    dve.wait_ge(b_ready, 2 * h + m + 1)
                    dve.tensor_tensor_scan(hT[:, m, half(h)], aT[:, m, half(h)], bT[:, m, half(h)], 0.0,
                                           ALU.mult, ALU.add).then_inc(h_ready, 1)
            for h in range(2):
                bs = slice(h * BH, (h + 1) * BH)

                def over(r):
                    return rowv[0:S, r, :].unsqueeze(1).to_broadcast([S, BH, D])

                for n in range(2):
                    dve.wait_ge(z_done, 2 * h + n + 1)
                    zb = slice(h * BH + 2 * n, h * BH + 2 * n + 2)
                    did(dve.tensor_tensor(zt[:, zb, :], bank[0:S, ZB[h] + n, :].rearrange("s (b d) -> s b d", b=2),
                                          bsum[:, :].unsqueeze(1).to_broadcast([S, 2, D]), ALU.add))
                sync()
                did(dve.tensor_tensor(zt[:, bs, :], zt[:, bs, :], over(R_HEAD), ALU.mult))
                sync()
                statistics(1, h, zt)
                normalize(1, h, zt, xn)
                did(dve.tensor_tensor(xn[:, bs, :], xn[:, bs, :], over(R_G), ALU.mult))
                sync()
                did(dve.tensor_tensor(xn[:, bs, :], xn[:, bs, :], over(R_B), ALU.add))
                sync()
                dve.tensor_tensor(xn[:, bs, :], xn[:, bs, :], zt[:, bs, :], ALU.add).then_inc(u_ready, 1)
            for h in range(2):
                dve.wait_ge(turned_out, 2 + h + 1)
                did(dve.tensor_copy(uhi[:, :, half(h)], uT[:, :, half(h)]))
                sync()
                dve.tensor_tensor(ulo[:, :, half(h)], uT[:, :, half(h)], uhi[:, :, half(h)].bitcast(F32),
                                  ALU.subtract).then_inc(u_split, 1)
            for n in range(NF):
                dve.wait_ge(gelu_ready, n + 1)
                if n >= 2:
                    dve.wait_ge(f2_done, n - 1)
                dve.tensor_copy(fhi[:, n % 2, :], fT[:, n % 2, :]).then_inc(f_split, 1)
                dve.wait_ge(f_split, 2 * n + 1)
                dve.tensor_tensor(flo[:, n % 2, :], fT[:, n % 2, :], fhi[:, n % 2, :].bitcast(F32),
                                  ALU.subtract).then_inc(f_split, 1)
            dve.wait_ge(f2_done, NF)
            for m in range(KB):
                dve.scalar_tensor_tensor(hT[:, m, :].rearrange("p (h t) -> p h t", h=2), pair(4 + 2 * m),
                                         cols[:, C_F2 + m:C_F2 + m + 1],
                                         uT[:, m, :].rearrange("p (h t) -> p h t", h=2),
                                         ALU.add, ALU.add).then_inc(v_ready, 1)
            for h in range(2):
                for n in range(2):
                    dve.wait_ge(p_done, 2 * h + n + 1)
                    xb = slice(h * BH + 2 * n, h * BH + 2 * n + 2)
                    did(dve.tensor_tensor(xs[:, xb, :], bank[0:S, 2 * h + n, :].rearrange("s (b d) -> s b d", b=2),
                                          xpb[:, xb, :], ALU.add))
                sync()
                statistics(2, h, xs)
                normalize(2, h, xs, xn)
                dve.sem_inc(norm_ready, 1)
            for h in range(2):
                for m in range(KB):
                    dve.wait_ge(q_done, 2 * h + m + 1)
                    dve.tensor_scalar(qf[:, m, half(h)], bank[:, 2 * h + m, 0:HALF], cols[:, C_Q + m:C_Q + m + 1],
                                      float(DH) ** -0.5, ALU.add, ALU.mult).then_inc(q_float, 1)
                dve.wait_ge(q_float, 2 * h + 2)
                did(dve.tensor_copy(qhi[:, :, half(h)], qf[:, :, half(h)]))
                sync()
                dve.tensor_tensor(qlo[:, :, half(h)], qf[:, :, half(h)], qhi[:, :, half(h)].bitcast(F32),
                                  ALU.subtract).then_inc(q_ready, 1)

            dve.wait_ge(q_ready, 2)
            dve.tensor_copy(irep[:, :, :], ident[0:S, 0:S].unsqueeze(1).to_broadcast([S, HG, S])).then_inc(att_consts, 1)
            dve.memset(orec[:, :], -1.0).then_inc(att_consts, 1)
            dve.wait_ge(att_consts, 2)
            dve.tensor_copy(minus[:, :], orec[:, 0:1].to_broadcast([S, KT + 1])).then_inc(att_consts, 1)
            dve.memset(vs[:, :, :, :, DH:VW], 1.0).then_inc(att_consts, 1)
            dve.memset(khi[:, :, :, SK:SK + 1].bitcast(F32), 0.0).then_inc(att_consts, 1)

            def key_low(b, s, k):
                dve.wait_ge(khi_ready, KB * b + k + 1)
                dve.scalar_tensor_tensor(klo[:, s, k, 0:SK], bank[:, 7, 0:SK], cols[:, C_K + k:C_K + k + 1],
                                         khi[:, s, k, 0:SK].bitcast(F32), ALU.add, ALU.subtract).then_inc(kv_out, 1)

            def values(b, s, t):
                dve.wait_ge(kv_done, 5 * b + KB + t + 1)
                dve.tensor_tensor(vs[:, s, t, :, 0:DH], bank[0:KT, 7, 0:D].rearrange("t (h d) -> t h d", h=H),
                                  rowv[:, R_V, :].rearrange("t (h d) -> t h d", h=H), ALU.add).then_inc(kv_out, 1)

            def mask_bias(b, s, loads, first=False):
                dve.wait_ge(in_mask[s], loads)
                if not first:
                    at(dve, st_done, 6 * (b - 1))
                dve.tensor_scalar(mbias[:, s, 0:SK], mask_in[:, s, :], 0.0, MASKED, ALU.is_equal, ALU.mult)\
                   .then_inc(mb_ready, 1)
                dve.wait_ge(mb_ready, b + 1)
                dve.tensor_reduce(some[:, s, :], mbias[:, s, 0:SK].bitcast(F32), AX.X, ALU.max).then_inc(mb_some, 1)
                dve.wait_ge(mb_some, 2 * b + 1)
                dve.tensor_scalar(some[:, s, :], some[:, s, :], -1.0, None, ALU.is_ge).then_inc(mb_some, 1)

            def row_max(b, s, h):
                at_all(dve, (s_done, H * b + h + 1), (max_ready, H * b + h - 1),
                       *([(diag_ready, 2 * b - 2)] if h == 0 else []))
                dve.tensor_tensor_reduce(out=scored[:, h % 2, :], in0=bank[0:S, h % 2, 0:SK],
                                         in1=mbias[:, s, 0:SK].bitcast(F32), scale=1.0, scalar=3 * MASKED,
                                         op0=ALU.add, op1=ALU.max, accum_out=smax[:, s, h:h + 1])\
                   .then_inc(max_ready, 1)

            def output(b, s):
                at(dve, pv_done, 2 * b + 2)
                o = bank[0:S, 6, 0:H * VW].rearrange("s (h v) -> s h v", h=H)
                dve.reciprocal(orec[:, :], o[:, :, DH]).then_inc(o_step, 1)
                dve.wait_ge(o_step, 3 * b + 1)
                dve.tensor_scalar(osum[:, :], orec[:, :], some[:, s, :], None, ALU.mult).then_inc(o_step, 1)
                dve.wait_ge(o_step, 3 * b + 2)
                dve.tensor_tensor(att[:, :, :], o[:, :, 0:DH], osum[:, :].unsqueeze(2).to_broadcast([S, H, DH]),
                                  ALU.mult).then_inc(o_step, 1)
                dve.wait_ge(o_step, 3 * b + 3)
                xb = xs[:, bass.ds(b, 1), :].rearrange("s o d -> s (o d)")
                dve.tensor_tensor(xb, xb, att[:, :, :].rearrange("s h d -> s (h d)"), ALU.add).then_inc(o_out, 1)

            key_low(0, 0, 0)
            key_low(0, 0, 1)
            for t in range(NK):
                values(0, 0, t)
            mask_bias(0, 0, 16, True)
            for h in range(H):
                row_max(0, 0, h)

            def attend(b, s, before, more, loads):
                if more:
                    key_low(b + 1, 1 - s, 0)
                    key_low(b + 1, 1 - s, 1)
                if before:
                    output(b - 1, 1 - s)
                if more:
                    mask_bias(b + 1, 1 - s, loads)
                    for h in range(H):
                        row_max(b + 1, 1 - s, h)
                        if h in (2, 6, 10):
                            values(b + 1, 1 - s, h // 4)

            attend(0, 0, False, True, 16)
            with dve.Fori(0, 3) as i:
                for s in (1, 0):
                    b = 2 * i + 1 if s else 2 * i + 2
                    attend(b, s, True, True, 16 * (i + 2))
            attend(7, 1, True, False, None)
            output(7, 1)

            at(dve, o_out, B)
            for h in range(2):
                statistics(3, h, xs)
                normalize(3, h, xs, x3)
                dve.sem_inc(norm_ready, 1)
            for h in range(2):
                dve.wait_ge(turned_out, 6 + h + 1)
                did(dve.tensor_copy(x3hi[:, :, half(h)], x3T[:, :, half(h)]))
                sync()
                dve.tensor_tensor(x3lo[:, :, half(h)], x3T[:, :, half(h)], x3hi[:, :, half(h)].bitcast(F32),
                                  ALU.subtract).then_inc(x3_split, 1)
            dve.wait_ge(lg_done, 1)
            logits = bank[0:S, 4, 0:B * 2 * E].rearrange("s (b j e) -> s b j e", b=B, j=2)
            did(dve.tensor_reduce(lmax[:, :, :], logits, AX.X, ALU.max))
            sync()
            dve.tensor_tensor(lg[:, :, :, :].rearrange("s b j e -> s (b j) e"), logits.rearrange("s b j e -> s (b j) e"),
                              lmax[:, :, :].rearrange("s b j -> s (b j)").unsqueeze(2).to_broadcast([S, 2 * B, E]),
                              ALU.subtract).then_inc(lg_ready, 1)
            dve.wait_ge(soft_exp, 2)
            did(dve.tensor_reduce(lsum[:, :, :], lg[:, :, :, :], AX.X, ALU.add))
            sync()
            did(dve.reciprocal(lsum[:, :, :], lsum[:, :, :]))
            sync()
            did(dve.tensor_tensor(lg[:, :, :, :].rearrange("s b j e -> s (b j) e"),
                                  lg[:, :, :, :].rearrange("s b j e -> s (b j) e"),
                                  lsum[:, :, :].rearrange("s b j -> s (b j)").unsqueeze(2).to_broadcast([S, 2 * B, E]),
                                  ALU.mult))
            sync()
            did(dve.tensor_tensor(cw[:, :, :], lg[:, :, 0, :], lg[:, :, 1, :], ALU.mult))
            sync()
            did(dve.tensor_reduce(cws[:, :], cw[:, :, :], AX.X, ALU.add))
            sync()
            did(dve.tensor_scalar(cws[:, :], cws[:, :], 1e-9, None, ALU.add))
            sync()
            did(dve.reciprocal(cws[:, :], cws[:, :]))
            sync()
            dve.tensor_tensor(cw[:, :, :], cw[:, :, :], cws[:, :].unsqueeze(2).to_broadcast([S, B, E]),
                              ALU.mult).then_inc(cw_ready, 1)

            def hidden(e, n):
                f = 8 * e + n
                at(dve, silu_ready, f + 1)
                dve.wait_ge(u_done, f + 1)
                at(dve, h_split, f)
                dve.tensor_tensor(hid[:, :].rearrange("p (h t) -> p h t", h=2), pair(2),
                                  sg[:, n % 2, :].rearrange("p (h t) -> p h t", h=2), ALU.mult).then_inc(h_float, 1)
                at(dve, h_float, f + 1)
                at(dve, chunk_used, f - 1)
                dve.tensor_copy(hhi[:, n % 2, :], hid[:, :]).then_inc(hhi_ready, 1)
                dve.wait_ge(hhi_ready, f + 1)
                dve.tensor_tensor(hlo[:, n % 2, :], hid[:, :], hhi[:, n % 2, :].bitcast(F32),
                                  ALU.subtract).then_inc(h_split, 1)

            def weigh(e, first=False):
                at(dve, chunk_used, 8 * e + 8)
                for m in range(KB):
                    if not first:
                        at(dve, acc_done, KB * (e - 1) + m + 1)
                    dve.tensor_tensor(yw[:, m, :].rearrange("p (h t) -> p h t", h=2), pair(4 + 2 * m),
                                      cwb[:, bass.ds(e, 1), :].rearrange("p o (h t) -> p (o h) t", h=2),
                                      ALU.mult).then_inc(y_out, 1)

            for n in range(NF):
                hidden(0, n)
            dve.wait_ge(in_cw, 16)
            weigh(0, True)
            with dve.Fori(1, E) as e:
                for n in range(NF):
                    hidden(e, n)
                weigh(e)
            for n in range(4):
                dve.wait_ge(fin_done, n + 1)
                dve.tensor_tensor(xs[:, 2 * n:2 * n + 2, :], bank[0:S, n, :].rearrange("s (b d) -> s b d", b=2),
                                  xs[:, 2 * n:2 * n + 2, :], ALU.add).then_inc(fin_out, 1)

        @block.tensor
        def _(pe):
            begin(pe, st_done, pv_done, chunk_used)
            mm = pe.matmul

            def turn(n, src, h):
                for k in range(KB):
                    for b in range(BH):
                        ins = pe.transpose(bank[:, TB[n] + k, b * S:(b + 1) * S],
                                           src[:, h * BH + b, k * P:(k + 1) * P], ident[0:S, 0:S])
                ins.then_inc(turned, 1)

            pe.wait_ge(in_consts, 32)
            for h in range(2):
                pe.wait_ge(norm_ready, h + 1)
                if h:
                    pe.wait_ge(turned_out, 1)
                turn(h, xn, h)
            pe.wait_ge(in_ab, 16)
            for h in range(2):
                pe.wait_ge(turned_out, h + 1)
                for j, w in enumerate((W_A, W_B)):
                    for m in range(KB):
                        if h:
                            pe.wait_ge((a_ready, b_ready)[j], m + 1)
                        for k in range(KB):
                            ins = mm(bank[:, 2 + 2 * j + m, 0:HALF], wsq[:, w, k, m * P:(m + 1) * P],
                                     nT[:, k, half(h)], start=k == 0, stop=k == KB - 1)
                        ins.then_inc(ab_done, 1)
            pe.wait_ge(in_oc, 16)
            for h in range(2):
                pe.wait_ge(h_ready, 2 * h + 2)
                for b in range(BH):
                    o = bank[0:S, ZB[h] + b // 2, (b % 2) * D:(b % 2 + 1) * D]
                    for n, (src, w) in enumerate(((nT, W_O), (hT, W_C))):
                        for k in range(KB):
                            ins = mm(o, src[:, k, seq(h * BH + b)], wsq[:, w, k, :],
                                     start=(n, k) == (0, 0), stop=(n, k) == (1, KB - 1))
                    if b % 2:
                        ins.then_inc(z_done, 1)
            for h in range(2):
                pe.wait_ge(u_ready, h + 1)
                turn(2 + h, xn, h)

            def three_passes(outs, pairs):
                for o, ps in zip(outs, pairs):
                    n = 3 * len(ps)
                    i = 0
                    for whi_, wlo_, mhi, mlo in ps:
                        for w, m in ((whi_, mhi), (whi_, mlo), (wlo_, mhi)):
                            last = mm(o, w, m, start=i == 0, stop=i == n - 1)
                            i += 1
                return last

            def ff_down(n):
                pe.wait_ge(f_split, 2 * n + 2)
                for m in range(KB):
                    for h in range(2):
                        w = slice((n % 4) * D + m * P, (n % 4) * D + (m + 1) * P)
                        for i, (wt, a) in enumerate(((w2hi, fhi), (w2hi, flo), (w2lo, fhi))):
                            ins = mm(bank[:, 4 + 2 * m + h, 0:HALF], wt[:, n // 4, w], a[:, n % 2, half(h)],
                                     start=n == 0 and i == 0, stop=n == NF - 1 and i == 2)
                ins.then_inc(f2_done, 1)

            pe.wait_ge(u_split, 2)
            pe.wait_ge(ffw_lo, 4)
            for n in range(NF):
                if n >= 2:
                    pe.wait_ge(gelu_ready, n - 1)
                w = slice(n * P, (n + 1) * P)
                ins = three_passes([bank[:, 2 * (n % 2) + h, 0:HALF] for h in range(2)],
                                   [[(w1hi[:, k, w], w1lo[:, k, w], uhi[:, k, half(h)], ulo[:, k, half(h)])
                                     for k in range(KB)] for h in range(2)])
                ins.then_inc(f1_done, 1)
                if n:
                    ff_down(n - 1)
            ff_down(NF - 1)
            pe.wait_ge(in_pq, 16)
            pe.wait_ge(v_ready, 2)
            for h in range(2):
                for b in range(BH):
                    o = bank[0:S, 2 * h + b // 2, (b % 2) * D:(b % 2 + 1) * D]
                    for k in range(KB):
                        ins = mm(o, hT[:, k, seq(h * BH + b)], wsq[:, W_P, k, :], start=k == 0, stop=k == KB - 1)
                    if b % 2:
                        ins.then_inc(p_done, 1)
            for h in range(2):
                pe.wait_ge(norm_ready, 2 + h + 1)
                turn(4 + h, xn, h)
            for h in range(2):
                pe.wait_ge(turned_out, 4 + h + 1)
                for m in range(KB):
                    for k in range(KB):
                        ins = mm(bank[:, 2 * h + m, 0:HALF], wsq[:, W_Q, k, m * P:(m + 1) * P], nT[:, k, half(h)],
                                 start=k == 0, stop=k == KB - 1)
                    ins.then_inc(q_done, 1)

            def key_value(b, s, g, loads=None):
                if loads is not None:
                    pe.wait_ge(in_ctx[s], loads)
                at(pe, kv_out, 5 * b + g)
                for k in range(KB):
                    c = cxt[:, s, k, :]
                    if g < KB:
                        ins = mm(bank[:, 7, 0:SK], wsq[:, W_K, k, g * P:(g + 1) * P], c,
                                 start=k == 0, stop=k == KB - 1)
                    else:
                        t = g - KB
                        ins = mm(bank[0:KT, 7, 0:D], c[:, t * KT:(t + 1) * KT], wsq[:, W_V, k, :],
                                 start=k == 0, stop=k == KB - 1)
                ins.then_inc(kv_done, 1)

            def score(b, s, h):
                if h == 0:
                    at(pe, kv_out, 5 * b + 2)
                    pe.wait_ge(qb_ready, 4 * b + 4)
                at(pe, max_ready, H * b + h - 1)
                k, j = h // HH, h % HH
                mm(bank[0:S, h % 2, 0:SK + 1], qbh[:, s, k, j, :], khi[:, s, k, :], start=True, stop=True)\
                    .then_inc(s_done, 1)

            def scores_t(b, s, u, between):
                k, t = u // NK, u % NK
                at(pe, exp_done, 6 * b + u - 1)
                if t == 0:
                    at(pe, diag_ready, 2 * b + k + 1)
                ks = slice(t * KT, (t + 1) * KT)
                for g in range(2):
                    between(g)
                    o = bank[0:KT, 2 + 2 * (u % 2) + g, 0:HG * S]
                    qh = qbh[:, s, k, g * HG:(g + 1) * HG, :].rearrange("p h t -> p (h t)")
                    ql = qbl[:, s, k, g * HG:(g + 1) * HG, :].rearrange("p h t -> p (h t)")
                    dg = diag[:, k, g * HG:(g + 1) * HG, :].rearrange("p h t -> p (h t)")
                    mm(o, khi[:, s, k, ks], qh, start=True, stop=False)
                    mm(o, khi[:, s, k, ks], ql, start=False, stop=False)
                    mm(o, klo[:, s, k, ks], qh, start=False, stop=False)
                    mm(o, mbias[:, s, ks], irep[:, :, :].rearrange("p h t -> p (h t)"), start=False, stop=False)
                    ins = mm(o, minus[:, 0:KT], dg, start=False, stop=True)
                ins.then_inc(st_done, 1)

            def weighted(b, s, k, heads):
                if heads[0] == 0:
                    at(pe, exp_done, 6 * b + 3 * k + 3)
                    if k == 0:
                        at(pe, o_out, b)
                        at(pe, kv_out, 5 * b + 5)
                for j in heads:
                    h = k * HH + j
                    for t in range(NK):
                        ins = mm(bank[0:S, 6, h * VW:(h + 1) * VW], prob[:, k, t, j * S:(j + 1) * S],
                                 vs[:, s, t, h, :], start=t == 0, stop=t == NK - 1)
                if heads[-1] == HH - 1:
                    ins.then_inc(pv_done, 1)

            pe.wait_ge(in_kv, 16)
            pe.wait_ge(q_ready, 2)
            for g in range(5):
                key_value(0, 0, g, 16 if g == 0 else None)
            pe.wait_ge(att_consts, 5)
            pe.wait_ge(mb_ready, 1)
            for h in range(H):
                score(0, 0, h)

            def attend(b, s, before, more, loads):
                for u in range(6):
                    def next_score(i):
                        if more and u >= 2:
                            score(b + 1, 1 - s, 4 * (u - 2) + i)

                    scores_t(b, s, u, next_score)
                    next_score(2)
                    if u < 2 and before:
                        weighted(b - 1, 1 - s, 1, range(4 * u, 4 * u + 4))
                    if u >= 3:
                        weighted(b, s, 0, ((0, 1, 2), (3, 4, 5), (6, 7))[u - 3])
                    if more and u < 5:
                        key_value(b + 1, 1 - s, u, loads if u == 0 else None)
                    next_score(3)

            attend(0, 0, False, True, 16)
            with pe.Fori(0, 3) as i:
                for s in (1, 0):
                    b = 2 * i + 1 if s else 2 * i + 2
                    attend(b, s, True, True, 16 * (i + 2))
            attend(7, 1, True, False, None)
            weighted(7, 1, 1, range(HH))

            for h in range(2):
                pe.wait_ge(norm_ready, 4 + h + 1)
                turn(6 + h, x3, h)
            pe.wait_ge(in_router, 16)
            pe.wait_ge(turned_out, 8)
            for b in range(B):
                for k in range(KB):
                    ins = mm(bank[0:S, 4, b * 2 * E:(b + 1) * 2 * E], x3T[:, k, seq(b)], wrt[:, k, :],
                             start=k == 0, stop=k == KB - 1)
            ins.then_inc(lg_done, 1)

            def gate_up(e, n, j):
                f = 8 * e + n
                if j == 0:
                    at(pe, w_lo, f + 1)
                    at(pe, silu_ready, f)
                else:
                    at(pe, h_float, f)
                wh, wl = chunk(whi, n % RING, j), chunk(wlo, n % RING, j)
                ins = three_passes([bank[:, 2 * j + h, 0:HALF] for h in range(2)],
                                   [[(wh[:, k, :], wl[:, k, :], x3hi[:, k, half(h)], x3lo[:, k, half(h)])
                                     for k in range(KB)] for h in range(2)])
                ins.then_inc((g_done, u_done)[j], 1)

            def expert_down(e, n):
                at(pe, h_split, 8 * e + n + 1)
                if n == 0:
                    at(pe, y_out, KB * e)
                wh, wl = chunk(whi, n % RING, 2), chunk(wlo, n % RING, 2)
                for m in range(KB):
                    ms = slice(m * P, (m + 1) * P)
                    for h in range(2):
                        for i, (w, a) in enumerate(((wh, hhi), (wh, hlo), (wl, hhi))):
                            ins = mm(bank[:, 4 + 2 * m + h, 0:HALF], w[:, ms], a[:, n % 2, half(h)],
                                     start=n == 0 and i == 0, stop=n == NF - 1 and i == 2)
                ins.then_inc(chunk_used, 1)

            def expert(e, first=False):
                for n in range(NF):
                    gate_up(e, n, 0)
                    gate_up(e, n, 1)
                    if n:
                        expert_down(e, n - 1)
                    if first and n == 0:
                        pe.wait_ge(cw_ready, 1)
                        for b in range(B):
                            ins = pe.transpose(bank[0:E, 5 + b // BH, (b % BH) * S:(b % BH + 1) * S],
                                               cw[:, b, :], ident[0:S, 0:S])
                        ins.then_inc(cwT_done, 1)
                        pe.wait_ge(cwT_ready, 1)
                expert_down(e, NF - 1)

            pe.wait_ge(x3_split, 2)
            expert(0, True)
            with pe.Fori(1, E) as e:
                expert(e)
            for n in range(4):
                for m in range(KB):
                    at(pe, acc_done, KB * (E - 1) + m + 1)
                    for b in range(2):
                        ins = pe.transpose(bank[0:S, n, b * D + m * P:b * D + (m + 1) * P],
                                           acc[:, m, seq(2 * n + b)], ident)
                ins.then_inc(fin_done, 1)


def kernel(**inputs):
    import numpy as np
    import concourse.bacc as bacc
    from concourse.bass_utils import run_bass_kernel_spmd

    def get(name):
        return np.asarray(inputs[name])

    def block1(name):
        return get("L0_attn_" + name)

    def in_blocks(w):
        return w.reshape(-1, P, w.shape[1]).transpose(1, 0, 2)

    square = np.stack([in_blocks(w.T) for w in (
        block1("Wa_w"), block1("Wb_w"), block1("Wo_w"), block1("C_w"), block1("p_w"),
        get("L0_xattn_Wq"), get("L0_xattn_Wk"), get("L0_xattn_Wv"))], axis=1)
    columns = np.concatenate([v.reshape(-1, P).T for v in (
        block1("Wa_b"), block1("Wb_b"), get("L0_xattn_bq"), get("L0_xattn_bk"), block1("f1_b"), block1("f2_b"))], axis=1)
    rows = np.stack([block1("C_b"), block1("Wo_b"), np.repeat(block1("head_weights"), DH), block1("ln_g"),
                     block1("ln_b"), block1("p_b"), get("L0_xattn_bv")])
    heads = (np.arange(P)[:, None] // DH == np.arange(HH)[None, :])
    arrays = {
        "x": get("x").transpose(1, 0, 2),
        "context": get("ctx_1024").transpose(0, 2, 1).reshape(B, KB, P, SK).transpose(0, 2, 1, 3),
        "mask": get("mask_Bx1xSxS2_ik1").reshape(B, S, SK),
        "square": square,
        "ff1": in_blocks(block1("f1_w").T),
        "ff2": in_blocks(block1("f2_w").T),
        "columns": columns,
        "rows": rows,
        "router": np.concatenate([in_blocks(get("L0_ffn_w_router")), in_blocks(get("L0_ffn_w_gating"))], axis=2),
        "gate": get("L0_ffn_w_gate"),
        "up": get("L0_ffn_w_up"),
        "down": get("L0_ffn_w_down"),
        "constants": np.concatenate([np.eye(P), heads], axis=1).astype(np.float32),
    }
    arrays = {n: np.ascontiguousarray(a) for n, a in arrays.items()}
    nc = bacc.Bacc("TRN2", target_bir_lowering=False, num_devices=1)
    args = [nc.dram_tensor(n, a.shape, mybir.dt.from_np(a.dtype), kind="ExternalInput").ap() for n, a in arrays.items()]
    y = nc.dram_tensor("y", (B, S, D), F32, kind="ExternalOutput").ap()
    decoder_layer(nc, *args, y)
    got = run_bass_kernel_spmd(nc, [arrays], core_ids=[0])
    return got.results[0]["y"]
```

```python
import concourse.bass as bass
from concourse import mybir
from contextlib import ExitStack

F32 = mybir.dt.float32
F32R = mybir.dt.float32r
I32 = mybir.dt.int32
ALU = mybir.AluOpType
ACT = mybir.ActivationFunctionType
AX = mybir.AxisListType

B, S, D = 8, 112, 256
SK = 375
H, DH = 16, 16
P = 128
KB = D // P
T = B * S
HALF = T // 2
BH = B // 2
FF = 1024
NF = FF // P
E = 8
KT, NK = 125, 3
HH = H // KB
HG = 4
NG = H // HG
GP = HG * DH
MR = S + HH
VW = DH + 1
RING = 4
LEAD = RING - 1
LN_EPS = 1e-5
MASKED = -1e30
W_A, W_B, W_O, W_C, W_P, W_Q, W_K, W_V = range(8)
C_A, C_B, C_Q, C_K, C_F1, C_F2 = 0, 2, 4, 6, 8, 16
R_C, R_O, R_HEAD, R_G, R_B, R_P, R_V = range(7)
GATE_SCALE = 10.0 / (1.0 + 1.4901161193847656e-08)
TB = ((0, 1), (6, 7), (4, 5), (2, 3), (6, 7), (4, 5), (0, 1), (7, 1))
ZB, FB, PB, QB = (0, 2), (4, 2), (4, 2), (4, 2)
BESIDE = (2 * B * D + 4 * KB * T + BH * D + D + 6 * HALF + NF * D
          - (KB * HH * S + KB * NK * HH * S + 2 * NG * HG * S + 2 * H + H * DH
             + 2 * (SK + 1) + KB * MR + 2 * SK + KB * S + B * D + KB * T))
UNDER_X3 = (2 * B * D + 4 * KB * T + BH * D + D + 6 * HALF + NF * D - BESIDE
            - (E * T + 5 * T + B * 2 * E + 4 * B + B * E + B + T))
LN3_PARTS = (slice(0, BH), slice(BH, B - 1), slice(B - 1, B))
LAG = 2


def decoder_layer(nc, x, context, mask, square, ff1, ff2, columns, rows, router, gate, up, down, constants, out):
    ctx = ExitStack()
    with ctx:
        def sb(name, shape, dt=F32, to=ctx):
            return to.enter_context(nc.sbuf_tensor(name, shape, dt))

        def sem(name):
            return ctx.enter_context(nc.semaphore(name))

        xs = sb("xs", [S, B, D])
        consts = sb("consts", [P, P + HG + HH])
        cols = sb("cols", [P, 18])
        rowv = sb("rowv", [KT, 7, D])
        wsq = sb("wsq", [P, 8, KB, D])
        wrt = sb("wrt", [P, KB, 2 * E])
        stats = sb("stats", [S, 4, B, 6])
        mv = sb("mv", [S, 4, B, 2])
        var = sb("var", [S, 4, B])
        rstd = sb("rstd", [S, 4, B])
        nhalf = sb("nhalf", [S, B])
        raw = sb("raw", [P, 2, 12 * D])
        ffw = ctx.enter_context(ExitStack())
        w1hi = sb("w1hi", [P, 2, KB * FF // 2], F32R, to=ffw)
        w1lo = sb("w1lo", [P, 2, KB * FF // 2], F32R, to=ffw)
        w2hi = sb("w2hi", [P, 2, NF // 2 * D], F32R, to=ffw)
        ffw.close()
        whi = sb("whi", [P, RING, 6 * P], F32R)
        wlo = sb("wlo", [P, RING, 6 * P], F32R)
        qhl = sb("qhl", [P, 2, KB, T], F32R)
        qhi, qlo = qhl[:, 0, :, :], qhl[:, 1, :, :]
        ident = consts[:, 0:P]
        headmask = consts[:, P:P + HG]
        rowmask = consts[:, P + HG:P + HG + HH]
        cw_dram = nc.dram_tensor("cw_dram", (E, T), F32, kind="Internal").ap()
        bank = ctx.enter_context(nc.psum_tensor("bank", [P, 8, 512], F32))

        one = ctx.enter_context(ExitStack())
        zt = sb("zt", [S, B, D], to=one)
        xn = sb("xn", [S, B, D], to=one)
        nT = sb("nT", [P, KB, T], to=one)
        aT = sb("aT", [P, KB, T], to=one)
        bT = sb("bT", [P, KB, T], to=one)
        hT = sb("hT", [P, KB, T], to=one)
        uT, qf = aT, bT
        uhi, ulo = qhi, qlo
        zb = sb("zb", [S, BH, D], to=one)
        bsum = sb("bsum", [S, D], to=one)
        fT = sb("fT", [P, 2, HALF], to=one)
        fhi = sb("fhi", [P, 2, HALF], F32R, to=one)
        flo = sb("flo", [P, 2, HALF], F32R, to=one)
        w2lo = sb("w2lo", [P, 2, NF // 2 * D], F32R, to=one)
        one.close()

        two = ctx.enter_context(ExitStack())
        weighed = sb("weighed", [MR, KB, HH, S], F32R, to=two)
        prob = sb("prob", [KT, KB, NK, HH * S], to=two)
        qb = [[], []]
        for part in ("high", "low"):
            qb[1].append(sb(f"qb1_{part}", [P, NG, HG, S], F32R, to=two))
        osum = sb("osum", [S, H], to=two)
        orec = sb("orec", [S, H], to=two)
        att = sb("att", [S, H, DH], to=two)
        smaxT = sb("smaxT", [MR, KB, S], to=two)
        mbias = sb("mbias", [MR, 2, SK + 1], F32R, to=two)
        smax = sb("smax", [S, KB, MR], to=two)
        scored = sb("scored", [S, 2, SK], to=two)
        x3 = sb("x3", [S, B, D], to=two)
        x3T = sb("x3T", [P, KB, T], to=two)
        sb("beside", [P, BESIDE], to=two)
        for part in ("high", "low"):
            qb[0].append(sb(f"qb0_{part}", [P, NG, HG, S], F32R, to=two))
        cxt = sb("cxt", [P, 2, KB, SK], to=two)
        keys = sb("keys", [P, 2, NG, SK + 1], F32R, to=two)
        qboth = sb("qboth", [P, 2, NG, S], to=two)
        vs = sb("vs", [KT, 2, NK, H, VW], to=two)
        mask_in = sb("mask_in", [S, 2, SK], I32, to=two)
        some = sb("some", [S, 2, 1], to=two)
        two.close()

        three = ctx.enter_context(ExitStack())
        x3hi, x3lo = qhi, qlo
        cwb = sb("cwb", [P, E, T], to=three)
        sg = sb("sg", [P, 2, T], to=three)
        hid = sb("hid", [P, T], to=three)
        hhi = sb("hhi", [P, 2, T], F32R, to=three)
        lg = sb("lg", [S, B, 2, E], to=three)
        lmax = sb("lmax", [S, B, 2], to=three)
        lsum = sb("lsum", [S, B, 2], to=three)
        cw = sb("cw", [S, B, E], to=three)
        cws = sb("cws", [S, B], to=three)
        cwT = sb("cwT", [E, T], to=three)
        sb("under_x3", [P, UNDER_X3], to=three)
        hlo = sb("hlo", [P, 2, T], F32R, to=three)
        yw = sb("yw", [P, KB, T], to=three)
        acc = sb("acc", [P, KB, T], to=three)
        three.close()

        in_x = [sem(f"in_x{n}") for n in range(2)]
        in_consts, in_rows, in_ab, in_oc, in_pq, in_kv, in_router = map(
            sem, ("in_consts", "in_rows", "in_ab", "in_oc", "in_pq", "in_kv", "in_router"))
        in_ff = [sem(f"in_ff{n}") for n in range(2)]
        in_ctx = [sem(f"in_ctx{n}") for n in range(2)]
        in_mask = [sem(f"in_mask{n}") for n in range(2)]
        in_w = [sem(f"in_w{n}") for n in range(2)]
        out_cw, in_cw, out_done = sem("out_cw"), sem("in_cw"), sem("out_done")
        var_ready, rstd_ready, norm_ready = sem("var_ready"), sem("rstd_ready"), sem("norm_ready")
        dve_step = sem("dve_step")
        pool_step = sem("pool_step")
        turned, turned_out = sem("turned"), sem("turned_out")
        ab_done, a_ready, b_ready, h_ready = sem("ab_done"), sem("a_ready"), sem("b_ready"), sem("h_ready")
        z_done, z_ready, zb_ready, u_ready = sem("z_done"), sem("z_ready"), sem("zb_ready"), sem("u_ready")
        ffw_hi, ffw_lo, u_split = sem("ffw_hi"), sem("ffw_lo"), sem("u_split")
        fhi_ready = sem("fhi_ready")
        f1_done, gelu_ready, f_split, f2_done, v_ready = (
            sem("f1_done"), sem("gelu_ready"), sem("f_split"), sem("f2_done"), sem("v_ready"))
        p_done, x1_ready, q_done, q_float, q_ready = (
            sem("p_done"), sem("x1_ready"), sem("q_done"), sem("q_float"), sem("q_ready"))
        kv_done, khi_ready, kv_out, mb_ready, mb_some = (
            sem("kv_done"), sem("khi_ready"), sem("kv_out"), sem("mb_ready"), sem("mb_some"))
        qboth_ready, qb_ready, s_done, max_ready = (
            sem("qboth_ready"), sem("qb_ready"), sem("s_done"), sem("max_ready"))
        maxT_done, maxT_out, weighed_ready = sem("maxT_done"), sem("maxT_out"), sem("weighed_ready")
        st_done, exp_done, pv_done, o_out, o_step = (
            sem("st_done"), sem("exp_done"), sem("pv_done"), sem("o_out"), sem("o_step"))
        att_consts = sem("att_consts")
        passed = sem("passed")
        x3_float, x3_split, lg_done, soft_exp, lg_ready, cw_ready, cwT_done, cwT_ready = map(
            sem, ("x3_float", "x3_split", "lg_done", "soft_exp", "lg_ready", "cw_ready", "cwT_done", "cwT_ready"))
        w_hi, w_lo, g_done, u_done, silu_ready, h_float, hhi_ready, h_split = map(
            sem, ("w_hi", "w_lo", "g_done", "u_done", "silu_ready", "h_float", "hhi_ready", "h_split"))
        chunk_used, y_out, acc_done, fin_done, fin_out = map(
            sem, ("chunk_used", "y_out", "acc_done", "fin_done", "fin_out"))

        START = ((st_done, 4), (kv_out, 1), (max_ready, 2), (exp_done, 2), (pv_done, 2), (o_out, 1),
                 (maxT_done, 1), (maxT_out, 2), (weighed_ready, 4), (chunk_used, RING), (silu_ready, 1), (h_float, 2), (h_split, 1),
                 (y_out, 1), (acc_done, 1))

        def started(s):
            return sum(n for other, n in START if other is s)

        def at(eng, s, count):
            eng.wait_ge(s, count + started(s))

        def at_all(eng, *counts):
            for s, n in counts:
                at(eng, s, n)
                eng.sem_inc(passed, 1)

        def begin(eng, *sems):
            for s in sems:
                eng.sem_inc(s, started(s))

        def half(b):
            return slice(b * HALF, (b + 1) * HALF)

        def seq(b):
            return slice(b * S, (b + 1) * S)

        def pair(n):
            return bank[:, n:n + 2, 0:HALF]

        gate_v = gate.rearrange("e (k p) f -> e p k f", p=P)
        up_v = up.rearrange("e (k p) f -> e p k f", p=P)
        down_v = down.rearrange("e (n p) d -> e p n d", p=P)

        def raw_part(slot, what):
            if what < 2:
                return raw[:, slot, what * 4 * D:(what + 1) * 4 * D].rearrange("p (k f) -> p k f", k=KB)
            return raw[:, slot, 8 * D:12 * D].rearrange("p (n d) -> p n d", n=4)

        def raw_chunk(slot, n, what):
            if what < 2:
                return raw_part(slot, what)[:, :, n * P:(n + 1) * P]
            return raw_part(slot, 2)[:, n, :]

        def chunk(w, r, what):
            part = w[:, r, what * 2 * P:(what + 1) * 2 * P]
            return part.rearrange("p (k f) -> p k f", k=KB) if what < 2 else part

        block = ctx.enter_context(nc.Block())

        @block.sync
        def _(sp):
            xv = x.rearrange("s (n b) d -> n s b d", n=2)
            sp.dma_start(xs[:, 0:BH, :], xv[0]).then_inc(in_x[0], 16)
            sp.dma_start(consts[:, :], constants).then_inc(in_consts, 16)
            sp.dma_start(cols[:, :], columns).then_inc(in_consts, 16)
            sp.dma_start(xs[:, BH:B, :], xv[1]).then_inc(in_x[1], 16)
            sp.dma_start(wsq[:, W_A:W_B + 1, :, :], square[:, W_A:W_B + 1, :, :]).then_inc(in_ab, 16)
            sp.dma_start(wsq[:, W_O:W_C + 1, :, :], square[:, W_O:W_C + 1, :, :]).then_inc(in_oc, 16)
            sp.dma_start(rowv[:, :, :], rows.rearrange("r d -> (r d)").partition_broadcast(KT)
                         .rearrange("s (r d) -> s r d", r=7)).then_inc(in_rows, 16)
            sp.dma_start(raw[:, 0, 0:KB * FF], ff1.rearrange("p k f -> p (k f)")).then_inc(in_ff[0], 16)
            sp.dma_start(raw[:, 1, 0:NF * D], ff2.rearrange("p n d -> p (n d)")).then_inc(in_ff[1], 16)
            sp.dma_start(wsq[:, W_K:W_V + 1, :, :], square[:, W_K:W_V + 1, :, :]).then_inc(in_kv, 16)

            def load_experts(e, s):
                f = slice(s * FF // 2, (s + 1) * FF // 2)
                n = slice(s * NF // 2, (s + 1) * NF // 2)
                sp.dma_start(raw_part(s, 0), gate_v[e, :, :, f]).then_inc(in_w[s], 16)
                sp.dma_start(raw_part(s, 1), up_v[e, :, :, f]).then_inc(in_w[s], 16)
                sp.dma_start(raw_part(s, 2), down_v[e, :, n, :]).then_inc(in_w[s], 16)

            def load_batch(b, s):
                sp.dma_start(cxt[:, s, :, :], context[b]).then_inc(in_ctx[s], 16)
                sp.dma_start(mask_in[:, s, :], mask[b]).then_inc(in_mask[s], 16)

            load_batch(0, 0)
            sp.dma_start(wsq[:, W_P:W_Q + 1, :, :], square[:, W_P:W_Q + 1, :, :]).then_inc(in_pq, 16)
            load_batch(1, 1)
            sp.dma_start(wrt[:, :, :], router).then_inc(in_router, 16)
            sp.wait_ge(ffw_hi, 4)
            sp.wait_ge(ffw_lo, 4)
            load_experts(0, 0)
            load_experts(0, 1)
            with sp.Fori(0, 3) as i:
                for s in range(2):
                    at_all(sp, (kv_done, 5 * (2 * i + s) + 5), (mb_ready, 2 * i + s + 1))
                    load_batch(2 * i + 2 + s, s)
            sp.wait_ge(cwT_ready, 1)
            sp.dma_start(cw_dram, cwT[:, :]).then_inc(out_cw, 16)
            sp.wait_ge(out_cw, 16)
            sp.dma_start(cwb[:, :, :].rearrange("p e t -> p (e t)"),
                         cw_dram.rearrange("e t -> (e t)").partition_broadcast(P)).then_inc(in_cw, 16)
            with sp.Fori(1, E) as e:
                for s in range(2):
                    at_all(sp, (w_hi, 8 * (e - 1) + 4 * s + 4), (w_lo, 8 * (e - 1) + 4 * s + 4))
                    load_experts(e, s)
            ov = out.rearrange("b s d -> s b d")
            for n in range(4):
                sp.wait_ge(fin_out, n + 1)
                sp.dma_start(ov[:, 2 * n:2 * n + 2, :], xs[:, 2 * n:2 * n + 2, :]).then_inc(out_done, 16)
            sp.wait_ge(out_done, 64)

        @block.gpsimd
        def _(pool):
            count = [0]

            def link(ins):
                count[0] += 1
                ins.then_inc(pool_step, 1)
                pool.wait_ge(pool_step, count[0])

            begin(pool, weighed_ready, acc_done)
            link(pool.memset(nhalf[:, :], -0.5))

            def rsqrt(ln, part, bs=None):
                pool.wait_ge(var_ready, 2 * ln + part + 1)
                bs = bs or slice(part * BH, (part + 1) * BH)
                pool.tensor_tensor(rstd[:, ln, bs], var[:, ln, bs], nhalf[:, bs], ALU.pow).then_inc(rstd_ready, 1)

            rsqrt(0, 0)
            rsqrt(0, 1)
            def weight_low(n, c):
                hi, lo = ((w1hi, w1lo), (w2hi, w2lo))[n]
                pool.wait_ge(ffw_hi, 2 * n + c + 1)
                pool.tensor_tensor(lo[:, c, :], raw[:, n, c * FF:(c + 1) * FF], hi[:, c, :].bitcast(F32),
                                   ALU.subtract).then_inc(ffw_lo, 1)

            def add_ln_b(h):
                pool.wait_ge(z_ready, h + 1)
                if h:
                    pool.wait_ge(u_ready, h)
                pool.tensor_tensor(zb[:, :, :], zt[:, h * BH:(h + 1) * BH, :],
                                   rowv[0:S, R_B, :].unsqueeze(1).to_broadcast([S, BH, D]), ALU.add)\
                    .then_inc(zb_ready, 1)

            def hidden_low(f):
                pool.wait_ge(fhi_ready, f + 1)
                pool.tensor_tensor(flo[:, f % 2, :], fT[:, f % 2, :], fhi[:, f % 2, :].bitcast(F32),
                                   ALU.subtract).then_inc(f_split, 1)

            weight_low(0, 0)
            weight_low(0, 1)
            weight_low(1, 0)
            add_ln_b(0)
            rsqrt(1, 0)
            weight_low(1, 1)
            add_ln_b(1)
            rsqrt(1, 1)
            for f in range(2 * NF):
                hidden_low(f)
                if f == NF + 4:
                    rsqrt(2, 0)

            def spread(b, s, k):
                pool.wait_ge(qboth_ready, b + 1)
                for part, dst in enumerate(qb[s]):
                    for g in (2 * k, 2 * k + 1):
                        q = qboth[:, part, g, :].unsqueeze(1).to_broadcast([P, HG, S])
                        m = headmask.unsqueeze(2).to_broadcast([P, HG, S])
                        pool.tensor_tensor(dst[:, g, :, :], q, m, ALU.mult).then_inc(qb_ready, 1)

            def weigh_rows(b, k, first=False):
                at(pool, maxT_out, 2 * b + k + 1)
                if not first:
                    at(pool, st_done, 6 * (b - 1) + 3 * (k + 1))
                for i in range(2):
                    heads = slice(i * HG, (i + 1) * HG)
                    v = smaxT[:, k, :].unsqueeze(1).to_broadcast([MR, HG, S])
                    m = rowmask[0:MR, heads].unsqueeze(2).to_broadcast([MR, HG, S])
                    pool.tensor_tensor(weighed[:, k, heads, :], v, m, ALU.mult).then_inc(weighed_ready, 1)

            spread(0, 0, 0)
            rsqrt(2, 1)
            spread(0, 0, 1)
            weigh_rows(0, 0, True)

            def attend(b, s):
                at(pool, st_done, 6 * (b - 1) + 3)
                spread(b + 1, 1 - s, 0)
                weigh_rows(b, 1)
                at(pool, st_done, 6 * b)
                spread(b + 1, 1 - s, 1)
                weigh_rows(b + 1, 0)

            def split_low(e, n):
                at(pool, w_hi, 8 * e + n + 1)
                for what in range(3):
                    ins = pool.tensor_tensor(chunk(wlo, n % RING, what), raw_chunk(n // 4, n % 4, what),
                                             chunk(whi, n % RING, what).bitcast(F32), ALU.subtract)
                ins.then_inc(w_lo, 1)

            with pool.Fori(0, 3) as i:
                for s in range(2):
                    attend(2 * i + s, s)
            attend(6, 0)
            rsqrt(3, 0)
            weigh_rows(B - 1, 1)
            rsqrt(3, 1, LN3_PARTS[1])
            for n in range(LEAD):
                split_low(0, n)
            rsqrt(3, 2, LN3_PARTS[2])

            def accumulate(e):
                for m in range(KB):
                    at(pool, y_out, KB * e + m + 1)
                    at(pool, acc_done, KB * e + m)
                    pool.tensor_tensor(acc[:, m, :], acc[:, m, :], yw[:, m, :], ALU.add).then_inc(acc_done, 1)

            at(pool, o_out, B)
            link(pool.memset(acc[:, :, :], 0.0))
            for n in range(LEAD, NF):
                split_low(0, n)
            for n in range(LEAD):
                split_low(1, n)

            def expert(e, more):
                accumulate(e - 1)
                for n in range(LEAD, NF):
                    split_low(e, n)
                if more:
                    for n in range(LEAD):
                        split_low(e + 1, n)

            with pool.Fori(1, E - 1) as e:
                expert(e, True)
            expert(E - 1, False)
            accumulate(E - 1)

        @block.scalar
        def _(act):
            begin(act, exp_done, maxT_out, silu_ready)

            def turn_out(n, dst):
                act.wait_ge(turned, n + 1)
                if TB[n][1] == TB[n][0] + 1:
                    ins = act.activation(dst, pair(TB[n][0]), ACT.Copy)
                else:
                    for k in range(KB):
                        ins = act.activation(dst[:, k, :], bank[:, TB[n][k], 0:HALF], ACT.Copy)
                ins.then_inc(turned_out, 1)

            turn_out(0, nT[:, :, half(0)])
            turn_out(1, nT[:, :, half(1)])
            act.wait_ge(in_consts, 32)
            for h in range(2):
                for m in range(KB):
                    act.wait_ge(ab_done, 4 * h + m + 1)
                    act.activation(aT[:, m, half(h)], bank[:, 2 + m, 0:HALF], ACT.Tanh,
                                   bias=cols[:, C_A + m:C_A + m + 1]).then_inc(a_ready, 1)
            for n, hi in enumerate((w1hi, w2hi)):
                act.wait_ge(in_ff[n], 16)
                for c in range(2):
                    act.activation(hi[:, c, :], raw[:, n, c * FF:(c + 1) * FF], ACT.Copy).then_inc(ffw_hi, 1)

            def key_high(b, s, k, kbank=7):
                act.wait_ge(kv_done, 5 * b + k + 1)
                for i in range(2):
                    own = slice(i * GP, (i + 1) * GP)
                    ins = act.activation(keys[own, s, 2 * k + i, 0:SK], bank[own, kbank, 0:SK], ACT.Identity,
                                         bias=cols[own, C_K + k:C_K + k + 1])
                ins.then_inc(khi_ready, 1)

            key_high(0, 0, 0)
            act.wait_ge(h_ready, 4)
            turn_out(2, uT[:, :, half(0)])
            key_high(0, 0, 1, 6)

            def hidden_high(f):
                n = f % NF
                act.wait_ge(f1_done, f + 1)
                if f >= 2:
                    act.wait_ge(f_split, f - 1)
                act.activation(fT[:, f % 2, :], bank[:, f % 2, 0:HALF], ACT.Gelu,
                               bias=cols[:, C_F1 + n:C_F1 + n + 1]).then_inc(gelu_ready, 1)
                act.wait_ge(gelu_ready, f + 1)
                if f >= 2:
                    act.wait_ge(f2_done, f - 1)
                act.activation(fhi[:, f % 2, :], fT[:, f % 2, :], ACT.Copy).then_inc(fhi_ready, 1)

            for f in range(2 * NF):
                hidden_high(f)
                if f == 5:
                    turn_out(3, uT[:, :, half(1)])
                if f == NF + 6:
                    turn_out(4, nT[:, :, half(0)])

            def both(b):
                act.wait_ge(qb_ready, 8 * b)
                first_both(b)

            def first_both(b):
                for rows in (slice(0, GP), slice(GP, P)):
                    for i in range(2):
                        own = slice(i * GP, (i + 1) * GP)
                        ins = act.activation(qboth[rows, :, i:NG:2, :],
                                             qhl[own, :, :, bass.ds(b * S, S)].bitcast(F32), ACT.Copy)
                ins.then_inc(qboth_ready, 1)

            def max_out(b, k):
                at(act, maxT_done, 2 * b + k + 1)
                at(act, weighed_ready, 2 * (2 * b + k) - 2)
                act.activation(smaxT[:, k, :], bank[0:MR, 7, 0:S], ACT.Copy)\
                   .then_inc(maxT_out, 1)

            def exps(b, u):
                k, t = u // NK, u % NK
                at(act, st_done, 6 * b + u + 1)
                at(act, pv_done, 2 * b + k - 1)
                act.activation(prob[:, k, t, :].rearrange("p (g t) -> p g t", g=2),
                               bank[0:KT, 2 + 2 * (u % 2):4 + 2 * (u % 2), 0:HG * S], ACT.Exp).then_inc(exp_done, 1)

            act.wait_ge(q_ready, 1)
            first_both(0)
            turn_out(5, nT[:, :, half(1)])
            max_out(0, 0)
            act.wait_ge(q_ready, 2)

            def split_high(e, n):
                c = 8 * e + n
                if n % 4 == 0:
                    act.wait_ge(in_w[n // 4], 48 * (e + 1))
                at(act, chunk_used, c + 1 - RING)
                for what in range(3):
                    ins = act.activation(chunk(whi, n % RING, what), raw_chunk(n // 4, n % 4, what), ACT.Copy)
                ins.then_inc(w_hi, 1)

            def attend(b, s, more):
                if more:
                    key_high(b + 1, 1 - s, 0)
                exps(b, 0)
                if more:
                    both(b + 1)
                exps(b, 1)
                if not more:
                    split_high(0, 0)
                max_out(b, 1)
                exps(b, 2)
                if more:
                    key_high(b + 1, 1 - s, 1)
                exps(b, 3)
                if not more:
                    split_high(0, 1)
                    turn_out(6, x3T[:, :, half(0)])
                exps(b, 4)
                if more:
                    max_out(b + 1, 0)
                else:
                    split_high(0, 2)
                exps(b, 5)

            with act.Fori(0, 3) as i:
                for s in range(2):
                    attend(2 * i + s, s, True)
            attend(6, 0, True)
            attend(7, 1, False)

            turn_out(7, x3T[:, :, half(1)])
            act.wait_ge(lg_ready, 1)
            for j, scale in enumerate((1.0, GATE_SCALE)):
                act.activation(lg[:, :, j, :], lg[:, :, j, :], ACT.Exp, scale=scale).then_inc(soft_exp, 1)
            def silu(e, n):
                f = 8 * e + n
                act.wait_ge(g_done, f + 1)
                at(act, h_float, f - 1)
                act.activation(sg[:, n % 2, :].rearrange("p (h t) -> p h t", h=2), pair(0), ACT.Silu)\
                   .then_inc(silu_ready, 1)

            def weights_out():
                act.wait_ge(cwT_done, 1)
                act.activation(cwT[:, :].rearrange("e (h t) -> e h t", h=2), bank[0:E, 6:8, 0:HALF], ACT.Copy)\
               .then_inc(cwT_ready, 1)

            def expert(e, more, first=False):
                for n in range(NF):
                    silu(e, n)
                    if first and n == 1:
                        weights_out()
                    if n < NF - LEAD:
                        split_high(e, n + LEAD)
                    elif more:
                        split_high(e + 1, n + LEAD - NF)

            expert(0, True, True)
            with act.Fori(1, E - 1) as e:
                expert(e, True)
            expert(E - 1, False)

        @block.vector
        def _(dve):
            count = [0]

            def did(ins):
                count[0] += 1
                ins.then_inc(dve_step, 1)

            def sync():
                dve.wait_ge(dve_step, count[0])

            begin(dve, kv_out, max_ready, o_out, h_float, h_split, y_out)

            def sequences(h, bs):
                return range(bs.start, bs.stop) if bs else range(h * BH, (h + 1) * BH)

            def statistics(ln, h, src, bs=None):
                bs = sequences(h, bs)
                for b in bs:
                    did(dve.bn_stats(stats[:, ln, b, :], src[:, b, :]))
                sync()
                for b in bs:
                    did(dve.bn_aggr(mv[:, ln, b, :], stats[:, ln, b, :]))
                sync()
                dve.tensor_scalar(var[:, ln, bs.start:bs.stop], mv[:, ln, bs.start:bs.stop, 1], LN_EPS, None,
                                  ALU.add).then_inc(var_ready, 1)

            def normalize(ln, h, src, dst, bs=None):
                dve.wait_ge(rstd_ready, 2 * ln + h + 1)
                for b in sequences(h, bs):
                    did(dve.tensor_scalar(dst[:, b, :], src[:, b, :], mv[:, ln, b, 0:1], rstd[:, ln, b:b + 1],
                                          ALU.subtract, ALU.mult))
                sync()

            for h in range(2):
                dve.wait_ge(in_x[h], 16)
                statistics(0, h, xs)
                normalize(0, h, xs, xn)
                dve.sem_inc(norm_ready, 1)
            dve.wait_ge(in_rows, 16)
            did(dve.tensor_tensor(bsum[:, :], rowv[0:S, R_C, :], rowv[0:S, R_O, :], ALU.add))
            did(dve.tensor_tensor(xs[:, :, :], xs[:, :, :],
                                  rowv[0:S, R_P, :].unsqueeze(1).to_broadcast([S, B, D]), ALU.add))
            dve.wait_ge(in_consts, 32)
            dve.memset(vs[:, :, :, :, DH:VW], 1.0).then_inc(att_consts, 1)
            dve.memset(keys[:, :, :, SK:SK + 1].bitcast(F32), 0.0).then_inc(att_consts, 1)
            for h in range(2):
                for m in range(KB):
                    dve.wait_ge(ab_done, 4 * h + 2 + m + 1)
                    dve.tensor_scalar(bT[:, m, half(h)], bank[:, 4 + m, 0:HALF], cols[:, C_B + m:C_B + m + 1], None,
                                      ALU.add).then_inc(b_ready, 1)
                for m in range(KB):
                    dve.wait_ge(a_ready, 2 * h + m + 1)
                    first = aT[:, m, half(h)].rearrange("p (b t) -> p b t", b=BH)[:, :, 0:1]
                    did(dve.memset(first, 0.0))
                    sync()
                    dve.wait_ge(b_ready, 2 * h + m + 1)
                    dve.tensor_tensor_scan(hT[:, m, half(h)], aT[:, m, half(h)], bT[:, m, half(h)], 0.0,
                                           ALU.mult, ALU.add).then_inc(h_ready, 1)

            def key_low(b, s, k, kbank=7):
                dve.wait_ge(khi_ready, KB * b + k + 1)
                for i in range(2):
                    own, other = slice(i * GP, (i + 1) * GP), slice((1 - i) * GP, (2 - i) * GP)
                    ins = dve.scalar_tensor_tensor(
                        keys[other, s, 2 * k + i, 0:SK], bank[own, kbank, 0:SK], cols[own, C_K + k:C_K + k + 1],
                        keys[own, s, 2 * k + i, 0:SK].bitcast(F32), ALU.add, ALU.subtract)
                ins.then_inc(kv_out, 1)

            def values(b, s, t):
                dve.wait_ge(kv_done, 5 * b + KB + t + 1)
                dve.tensor_tensor(vs[:, s, t, :, 0:DH], bank[0:KT, 7, 0:D].rearrange("t (h d) -> t h d", h=H),
                                  rowv[:, R_V, :].rearrange("t (h d) -> t h d", h=H), ALU.add).then_inc(kv_out, 1)

            def z_of(h):
                for n in range(2):
                    dve.wait_ge(z_done, 2 * h + n + 1)
                    zs = slice(h * BH + 2 * n, h * BH + 2 * n + 2)
                    did(dve.tensor_tensor(zt[:, zs, :], bank[0:S, ZB[h] + n, :].rearrange("s (b d) -> s b d", b=2),
                                          bsum[:, :].unsqueeze(1).to_broadcast([S, 2, D]), ALU.add))
                sync()
                bs = slice(h * BH, (h + 1) * BH)
                did(dve.tensor_tensor(zt[:, bs, :], zt[:, bs, :],
                                      rowv[0:S, R_HEAD, :].unsqueeze(1).to_broadcast([S, BH, D]), ALU.mult))
                sync()
                dve.sem_inc(z_ready, 1)

            def u_of(h):
                statistics(1, h, zt)
                for b in range(h * BH, (h + 1) * BH):
                    did(dve.scalar_tensor_tensor(xn[:, b, :], zt[:, b, :], mv[:, 1, b, 0:1], rowv[0:S, R_G, :],
                                                 ALU.subtract, ALU.mult))
                sync()
                dve.wait_ge(rstd_ready, 2 + h + 1)
                dve.wait_ge(zb_ready, h + 1)
                for b in range(h * BH, (h + 1) * BH):
                    ins = dve.scalar_tensor_tensor(xn[:, b, :], xn[:, b, :], rstd[:, 1, b:b + 1],
                                                   zb[:, b - h * BH, :], ALU.mult, ALU.add)
                ins.then_inc(u_ready, 1)

            def split_u(h):
                dve.wait_ge(turned_out, 2 + h + 1)
                did(dve.tensor_copy(uhi[:, :, half(h)], uT[:, :, half(h)]))
                sync()
                dve.tensor_tensor(ulo[:, :, half(h)], uT[:, :, half(h)], uhi[:, :, half(h)].bitcast(F32),
                                  ALU.subtract).then_inc(u_split, 1)

            def v_of(h):
                dve.wait_ge(f2_done, NF * (h + 1))
                for m in range(KB):
                    dve.scalar_tensor_tensor(hT[:, m, half(h)], bank[:, FB[h] + m, 0:HALF],
                                             cols[:, C_F2 + m:C_F2 + m + 1], uT[:, m, half(h)],
                                             ALU.add, ALU.add).then_inc(v_ready, 1)

            def x1_of(h):
                for n in range(2):
                    dve.wait_ge(p_done, 2 * h + n + 1)
                    xb = slice(h * BH + 2 * n, h * BH + 2 * n + 2)
                    did(dve.tensor_tensor(xs[:, xb, :], bank[0:S, PB[h] + n, :].rearrange("s (b d) -> s b d", b=2),
                                          xs[:, xb, :], ALU.add))
                sync()
                statistics(2, h, xs)
                normalize(2, h, xs, xn)
                dve.sem_inc(norm_ready, 1)

            def query(h, m):
                dve.wait_ge(q_done, 2 * h + m + 1)
                dve.tensor_scalar(qf[:, m, half(h)], bank[:, QB[h] + m, 0:HALF], cols[:, C_Q + m:C_Q + m + 1],
                                  float(DH) ** -0.5, ALU.add, ALU.mult).then_inc(q_float, 1)

            def split_q(h):
                dve.wait_ge(q_float, 2 * h + 2)
                did(dve.tensor_copy(qhi[:, :, half(h)], qf[:, :, half(h)]))
                sync()
                dve.tensor_tensor(qlo[:, :, half(h)], qf[:, :, half(h)], qhi[:, :, half(h)].bitcast(F32),
                                  ALU.subtract).then_inc(q_ready, 1)

            z_of(0)
            u_of(0)
            z_of(1)
            split_u(0)
            key_low(0, 0, 0)
            key_low(0, 0, 1, 6)
            u_of(1)
            for t in range(NK):
                values(0, 0, t)
            split_u(1)
            v_of(0)
            x1_of(0)
            query(0, 0)
            query(0, 1)
            split_q(0)

            def mask_bias(b, s, loads, first=False):
                dve.wait_ge(in_mask[s], loads)
                if not first:
                    at(dve, st_done, 6 * (b - 1))
                dve.tensor_scalar(mbias[0:S, s, 0:SK], mask_in[:, s, :], 0.0, MASKED, ALU.is_equal, ALU.mult)\
                   .then_inc(mb_ready, 1)
                dve.wait_ge(mb_ready, b + 1)
                dve.tensor_reduce(some[:, s, :], mbias[0:S, s, 0:SK].bitcast(F32), AX.X, ALU.max).then_inc(mb_some, 1)
                dve.wait_ge(mb_some, 2 * b + 1)
                dve.tensor_scalar(some[:, s, :], some[:, s, :], -1.0, None, ALU.is_ge).then_inc(mb_some, 1)

            def row_max(b, s, h):
                at_all(dve, (s_done, H * b + h + 2), (max_ready, H * b + h),
                       *([(maxT_done, 2 * (b - 1) + h // HH + 1)] if h % HH == 0 else []))
                for i in range(2):
                    dve.tensor_tensor_reduce(out=scored[:, i, :], in0=bank[0:S, i, 0:SK],
                                             in1=mbias[0:S, s, 0:SK].bitcast(F32), scale=1.0, scalar=3 * MASKED,
                                             op0=ALU.add, op1=ALU.max,
                                             accum_out=smax[:, h // HH, S + h % HH + i:S + h % HH + i + 1])\
                       .then_inc(max_ready, 1)

            def output(b, s):
                at(dve, pv_done, 2 * b + 2)
                o = bank[0:S, 6, 0:H * VW].rearrange("s (h v) -> s h v", h=H)
                dve.reciprocal(orec[:, :], o[:, :, DH]).then_inc(o_step, 1)
                dve.wait_ge(o_step, 3 * b + 1)
                dve.tensor_scalar(osum[:, :], orec[:, :], some[:, s, :], None, ALU.mult).then_inc(o_step, 1)
                dve.wait_ge(o_step, 3 * b + 2)
                dve.tensor_tensor(att[:, :, :], o[:, :, 0:DH], osum[:, :].unsqueeze(2).to_broadcast([S, H, DH]),
                                  ALU.mult).then_inc(o_step, 1)
                dve.wait_ge(o_step, 3 * b + 3)
                xb = xs[:, bass.ds(b, 1), :].rearrange("s o d -> s (o d)")
                dve.tensor_tensor(xb, xb, att[:, :, :].rearrange("s h d -> s (h d)"), ALU.add).then_inc(o_out, 1)

            v_of(1)
            dve.tensor_copy(smax[:, :, 0:S], ident[0:S, 0:S].unsqueeze(1).to_broadcast([S, KB, S]))\
               .then_inc(att_consts, 1)
            dve.memset(mbias[96:MR, :, :].bitcast(F32), -1.0).then_inc(att_consts, 1)
            dve.wait_ge(att_consts, 4)
            mask_bias(0, 0, 16, True)
            x1_of(1)
            for n, h in enumerate(range(0, HH, 2)):
                row_max(0, 0, h)
                if n in (1, 2):
                    query(1, n - 1)
            split_q(1)

            def attend(b, s, before, loads):
                key_low(b + 1, 1 - s, 0)
                for h in (8, 10, 12, 14):
                    row_max(b, s, h)
                if before:
                    output(b - 1, 1 - s)
                mask_bias(b + 1, 1 - s, loads)
                key_low(b + 1, 1 - s, 1)
                row_max(b + 1, 1 - s, 0)
                values(b + 1, 1 - s, 0)
                row_max(b + 1, 1 - s, 2)
                row_max(b + 1, 1 - s, 4)
                values(b + 1, 1 - s, 1)
                row_max(b + 1, 1 - s, 6)
                values(b + 1, 1 - s, 2)

            attend(0, 0, False, 16)
            with dve.Fori(0, 3) as i:
                for s in (1, 0):
                    b = 2 * i + 1 if s else 2 * i + 2
                    attend(b, s, True, 16 * (i + 2))
            def ln3(part):
                normalize(3, part, xs, x3, LN3_PARTS[part])
                dve.sem_inc(norm_ready, 1)

            def split_x3(h):
                dve.wait_ge(turned_out, 6 + h + 1)
                did(dve.tensor_copy(x3hi[:, :, half(h)], x3T[:, :, half(h)]))
                sync()
                dve.tensor_tensor(x3lo[:, :, half(h)], x3T[:, :, half(h)], x3hi[:, :, half(h)].bitcast(F32),
                                  ALU.subtract).then_inc(x3_split, 1)

            at(dve, o_out, BH)
            statistics(3, 0, xs, LN3_PARTS[0])
            for h in range(HH, H, 2):
                row_max(B - 1, 1, h)
            ln3(0)
            output(B - 2, 0)
            at(dve, o_out, B - 1)
            statistics(3, 1, xs, LN3_PARTS[1])
            ln3(1)
            dve.wait_ge(qboth_ready, B)
            split_x3(0)
            output(B - 1, 1)
            at(dve, o_out, B)
            statistics(3, 2, xs, LN3_PARTS[2])
            ln3(2)
            split_x3(1)

            dve.wait_ge(lg_done, 1)
            logits = bank[0:S, 4, 0:B * 2 * E].rearrange("s (b j e) -> s b j e", b=B, j=2)
            did(dve.tensor_reduce(lmax[:, :, :], logits, AX.X, ALU.max))
            sync()
            dve.tensor_tensor(lg[:, :, :, :].rearrange("s b j e -> s (b j) e"), logits.rearrange("s b j e -> s (b j) e"),
                              lmax[:, :, :].rearrange("s b j -> s (b j)").unsqueeze(2).to_broadcast([S, 2 * B, E]),
                              ALU.subtract).then_inc(lg_ready, 1)
            dve.wait_ge(soft_exp, 2)
            did(dve.tensor_reduce(lsum[:, :, :], lg[:, :, :, :], AX.X, ALU.add))
            sync()
            did(dve.reciprocal(lsum[:, :, :], lsum[:, :, :]))
            sync()
            did(dve.tensor_tensor(lg[:, :, :, :].rearrange("s b j e -> s (b j) e"),
                                  lg[:, :, :, :].rearrange("s b j e -> s (b j) e"),
                                  lsum[:, :, :].rearrange("s b j -> s (b j)").unsqueeze(2).to_broadcast([S, 2 * B, E]),
                                  ALU.mult))
            sync()
            did(dve.tensor_tensor(cw[:, :, :], lg[:, :, 0, :], lg[:, :, 1, :], ALU.mult))
            sync()
            did(dve.tensor_reduce(cws[:, :], cw[:, :, :], AX.X, ALU.add))
            sync()
            did(dve.tensor_scalar(cws[:, :], cws[:, :], 1e-9, None, ALU.add))
            sync()
            did(dve.reciprocal(cws[:, :], cws[:, :]))
            sync()
            dve.tensor_tensor(cw[:, :, :], cw[:, :, :], cws[:, :].unsqueeze(2).to_broadcast([S, B, E]),
                              ALU.mult).then_inc(cw_ready, 1)

            def hidden(e, n):
                f = 8 * e + n
                at(dve, silu_ready, f + 1)
                dve.wait_ge(u_done, f + 1)
                at(dve, h_split, f)
                dve.tensor_tensor(hid[:, :].rearrange("p (h t) -> p h t", h=2), pair(2),
                                  sg[:, n % 2, :].rearrange("p (h t) -> p h t", h=2), ALU.mult).then_inc(h_float, 1)
                at(dve, h_float, f + 1)
                at(dve, chunk_used, f - 1)
                dve.tensor_copy(hhi[:, n % 2, :], hid[:, :]).then_inc(hhi_ready, 1)
                dve.wait_ge(hhi_ready, f + 1)
                dve.tensor_tensor(hlo[:, n % 2, :], hid[:, :], hhi[:, n % 2, :].bitcast(F32),
                                  ALU.subtract).then_inc(h_split, 1)

            def weigh(e, first=False):
                at(dve, chunk_used, 8 * e + 8)
                for m in range(KB):
                    if not first:
                        at(dve, acc_done, KB * (e - 1) + m + 1)
                    dve.tensor_tensor(yw[:, m, :].rearrange("p (h t) -> p h t", h=2), pair(4 + 2 * m),
                                      cwb[:, bass.ds(e, 1), :].rearrange("p o (h t) -> p (o h) t", h=2),
                                      ALU.mult).then_inc(y_out, 1)

            for n in range(NF):
                hidden(0, n)
            dve.wait_ge(in_cw, 16)
            weigh(0, True)
            with dve.Fori(1, E) as e:
                for n in range(NF):
                    hidden(e, n)
                weigh(e)
            for n in range(4):
                dve.wait_ge(fin_done, n + 1)
                dve.tensor_tensor(xs[:, 2 * n:2 * n + 2, :], bank[0:S, n, :].rearrange("s (b d) -> s b d", b=2),
                                  xs[:, 2 * n:2 * n + 2, :], ALU.add).then_inc(fin_out, 1)

        @block.tensor
        def _(pe):
            begin(pe, st_done, pv_done, maxT_done, chunk_used)
            mm = pe.matmul

            def turn(n, src, h, some=range(BH)):
                for k in range(KB):
                    for b in some:
                        ins = pe.transpose(bank[:, TB[n][k], b * S:(b + 1) * S],
                                           src[:, h * BH + b, k * P:(k + 1) * P], ident[0:S, 0:S])
                if some[-1] == BH - 1:
                    ins.then_inc(turned, 1)

            pe.wait_ge(in_consts, 32)
            for h in range(2):
                pe.wait_ge(norm_ready, h + 1)
                turn(h, xn, h)
            pe.wait_ge(in_ab, 16)
            for h in range(2):
                pe.wait_ge(turned_out, h + 1)
                for j, w in enumerate((W_A, W_B)):
                    for m in range(KB):
                        if h:
                            pe.wait_ge((a_ready, b_ready)[j], m + 1)
                        for k in range(KB):
                            ins = mm(bank[:, 2 + 2 * j + m, 0:HALF], wsq[:, w, k, m * P:(m + 1) * P],
                                     nT[:, k, half(h)], start=k == 0, stop=k == KB - 1)
                        ins.then_inc(ab_done, 1)
            pe.wait_ge(in_oc, 16)
            for h in range(2):
                pe.wait_ge(h_ready, 2 * h + 2)
                pe.wait_ge(turned_out, 2)
                for b in range(BH):
                    o = bank[0:S, ZB[h] + b // 2, (b % 2) * D:(b % 2 + 1) * D]
                    for n, (src, w) in enumerate(((nT, W_O), (hT, W_C))):
                        for k in range(KB):
                            ins = mm(o, src[:, k, seq(h * BH + b)], wsq[:, w, k, :],
                                     start=(n, k) == (0, 0), stop=(n, k) == (1, KB - 1))
                    if b % 2:
                        ins.then_inc(z_done, 1)
            def three_passes(outs, pairs):
                for o, ps in zip(outs, pairs):
                    n = 3 * len(ps)
                    i = 0
                    for whi_, wlo_, mhi, mlo in ps:
                        for w, m in ((whi_, mhi), (whi_, mlo), (wlo_, mhi)):
                            last = mm(o, w, m, start=i == 0, stop=i == n - 1)
                            i += 1
                return last

            def ff_up(f):
                h, n = divmod(f, NF)
                if f >= 2:
                    pe.wait_ge(gelu_ready, f - 1)
                w = slice(n * P, (n + 1) * P)
                three_passes([bank[:, f % 2, 0:HALF]],
                             [[(w1hi[:, k, w], w1lo[:, k, w], uhi[:, k, half(h)], ulo[:, k, half(h)])
                               for k in range(KB)]]).then_inc(f1_done, 1)

            def ff_down(f):
                h, n = divmod(f, NF)
                pe.wait_ge(f_split, f + 1)
                for m in range(KB):
                    w = slice((n % 4) * D + m * P, (n % 4) * D + (m + 1) * P)
                    for i, (wt, a) in enumerate(((w2hi, fhi), (w2hi, flo), (w2lo, fhi))):
                        ins = mm(bank[:, FB[h] + m, 0:HALF], wt[:, n // 4, w], a[:, f % 2, :],
                                 start=n == 0 and i == 0, stop=n == NF - 1 and i == 2)
                ins.then_inc(f2_done, 1)

            def p_of(h):
                pe.wait_ge(v_ready, 2 * h + 2)
                for b in range(BH):
                    o = bank[0:S, PB[h] + b // 2, (b % 2) * D:(b % 2 + 1) * D]
                    for k in range(KB):
                        ins = mm(o, hT[:, k, seq(h * BH + b)], wsq[:, W_P, k, :], start=k == 0, stop=k == KB - 1)
                    if b % 2:
                        ins.then_inc(p_done, 1)

            def turn_x1(h):
                pe.wait_ge(norm_ready, 2 + h + 1)
                turn(4 + h, xn, h)

            def query(h, m):
                pe.wait_ge(turned_out, 4 + h + 1)
                for k in range(KB):
                    ins = mm(bank[:, QB[h] + m, 0:HALF], wsq[:, W_Q, k, m * P:(m + 1) * P], nT[:, k, half(h)],
                             start=k == 0, stop=k == KB - 1)
                ins.then_inc(q_done, 1)

            def key_value(b, s, g, loads=None, turned_before=True, kbank=7):
                if loads is not None:
                    pe.wait_ge(in_ctx[s], loads)
                at(pe, kv_out, 5 * b + (g if kbank == 7 else 0))
                if g < KB and turned_before:
                    at(pe, maxT_out, 2 * b + g - 1)
                for k in range(KB):
                    c = cxt[:, s, k, :]
                    if g < KB:
                        ins = mm(bank[:, kbank, 0:SK], wsq[:, W_K, k, g * P:(g + 1) * P], c,
                                 start=k == 0, stop=k == KB - 1)
                    else:
                        t = g - KB
                        ins = mm(bank[0:KT, 7, 0:D], c[:, t * KT:(t + 1) * KT], wsq[:, W_V, k, :],
                                 start=k == 0, stop=k == KB - 1)
                ins.then_inc(kv_done, 1)

            pe.wait_ge(in_kv, 16)
            key_value(0, 0, 0, 16, False)
            pe.wait_ge(u_ready, 1)
            turn(2, xn, 0)
            key_value(0, 0, 1, None, False, 6)
            pe.wait_ge(u_split, 1)
            pe.wait_ge(ffw_lo, 4)
            for f in range(2 * NF + LAG):
                if f == NF:
                    pe.wait_ge(u_split, 2)
                if f < 2 * NF:
                    ff_up(f)
                if f >= LAG:
                    ff_down(f - LAG)
                if f in (3, 4, 5):
                    key_value(0, 0, f - 1, None, False)
                if f == 5:
                    pe.wait_ge(u_ready, 2)
                    turn(3, xn, 1)
                if f == NF + LAG:
                    pe.wait_ge(in_pq, 16)
                    p_of(0)
                if f == NF + 6:
                    turn_x1(0)
                if f == 2 * NF:
                    query(0, 0)
                    query(0, 1)
            p_of(1)

            def score(b, s, h):
                if h % HH == 0:
                    at(pe, kv_out, 5 * b + 1 + h // HH)
                    at(pe, qb_ready, 8 * b + h // HH * 4 + 2)
                at(pe, max_ready, H * b + h - 1)
                g, j = h // HG, h % HG
                mm(bank[0:S, h % 2, 0:SK + 1], qb[s][0][:, g, j, :], keys[:, s, g, :], start=True, stop=True)\
                    .then_inc(s_done, 1)

            def turn_max(b, k, last=False):
                at(pe, max_ready, H * b + HH * (k + 1))
                at(pe, kv_out, 5 * b + 5 + (k == 1 and not last))
                pe.transpose(bank[0:MR, 7, 0:S], smax[:, k, :], ident[0:S, 0:S])\
                  .then_inc(maxT_done, 1)

            def scores_t(b, s, u, i):
                k, t = u // NK, u % NK
                if i == 0:
                    at(pe, exp_done, 6 * b + u - 1)
                    if t == 0:
                        at(pe, qb_ready, 8 * b + 4 * k + 4)
                ks = slice(t * KT, (t + 1) * KT)
                o = bank[0:KT, 2 + 2 * (u % 2) + i, 0:HG * S]
                g = 2 * k + i
                mm(o, keys[:, s, g, ks], qb[s][0][:, g, :, :].rearrange("p h t -> p (h t)"), start=True, stop=False)
                mm(o, keys[:, s, g, ks], qb[s][1][:, g, :, :].rearrange("p h t -> p (h t)"), start=False, stop=False)
                if t == 0:
                    at(pe, weighed_ready, 2 * (2 * b + k) + i + 1)
                ins = mm(o, mbias[:, s, ks],
                         weighed[:, k, i * HG:(i + 1) * HG, :].rearrange("p h t -> p (h t)"), start=False, stop=True)
                if i:
                    ins.then_inc(st_done, 1)

            def weighted(b, s, k, heads):
                if heads[0] == 0:
                    at(pe, exp_done, 6 * b + 3 * k + 3)
                    if k == 0:
                        at(pe, o_out, b)
                        at(pe, kv_out, 5 * b + 5)
                for j in heads:
                    h = k * HH + j
                    for t in range(NK):
                        ins = mm(bank[0:S, 6, h * VW:(h + 1) * VW], prob[:, k, t, j * S:(j + 1) * S],
                                 vs[:, s, t, h, :], start=t == 0, stop=t == NK - 1)
                if heads[-1] == HH - 1:
                    ins.then_inc(pv_done, 1)

            pe.wait_ge(att_consts, 4)
            pe.wait_ge(mb_ready, 1)
            for n, h in enumerate(range(0, HH, 2)):
                score(0, 0, h)
                score(0, 0, h + 1)
                if n == 0:
                    turn_x1(1)
                if n in (1, 2):
                    query(1, n - 1)
            turn_max(0, 0)
            pe.wait_ge(q_ready, 2)

            def attend(b, s, before, more, loads):
                def pair(h):
                    score(b, s, h)
                    score(b, s, h + 1)

                def next_pair(h):
                    if more:
                        score(b + 1, 1 - s, h)
                        score(b + 1, 1 - s, h + 1)

                def next_group(g):
                    if more:
                        key_value(b + 1, 1 - s, g, loads if g == 0 else None)

                def former(*heads):
                    if before:
                        weighted(b - 1, 1 - s, 1, heads)

                def now(*heads):
                    weighted(b, s, 0, heads)

                next_group(0)
                scores_t(b, s, 0, 0)
                pair(8)
                scores_t(b, s, 0, 1)
                former(0)
                scores_t(b, s, 1, 0)
                former(1)
                pair(10)
                scores_t(b, s, 1, 1)
                former(2)
                former(3)
                pair(12)
                scores_t(b, s, 2, 0)
                former(4)
                pair(14)
                former(5)
                former(6)
                former(7)
                turn_max(b, 1, not more)
                scores_t(b, s, 2, 1)
                next_group(1)
                scores_t(b, s, 3, 0)
                next_pair(0)
                scores_t(b, s, 3, 1)
                if not more:
                    pe.wait_ge(norm_ready, 5)
                    turn(6, x3, 0)
                now(0)
                next_group(2)
                now(1)
                next_pair(2)
                scores_t(b, s, 4, 0)
                now(2)
                scores_t(b, s, 4, 1)
                next_pair(4)
                now(3)
                next_group(3)
                now(4)
                next_pair(6)
                scores_t(b, s, 5, 0)
                now(5)
                next_group(4)
                now(6)
                now(7)
                if more:
                    turn_max(b + 1, 0)
                scores_t(b, s, 5, 1)

            attend(0, 0, False, True, 16)
            with pe.Fori(0, 3) as i:
                for s in (1, 0):
                    b = 2 * i + 1 if s else 2 * i + 2
                    attend(b, s, True, True, 16 * (i + 2))
            attend(7, 1, True, False, None)
            pe.wait_ge(norm_ready, 6)
            pe.wait_ge(turned_out, 7)
            turn(7, x3, 1, range(BH - 1))
            weighted(7, 1, 1, range(HH))

            def gates(h):
                for b in range(h * BH, (h + 1) * BH):
                    for k in range(KB):
                        ins = mm(bank[0:S, 4, b * 2 * E:(b + 1) * 2 * E], x3T[:, k, seq(b)], wrt[:, k, :],
                                 start=k == 0, stop=k == KB - 1)
                if h:
                    ins.then_inc(lg_done, 1)

            def gate_up(e, n, j, halves=(0, 1)):
                f = 8 * e + n
                if halves[0] == 0:
                    if j == 0:
                        at(pe, w_lo, f + 1)
                        at(pe, silu_ready, f)
                    else:
                        at(pe, h_float, f)
                wh, wl = chunk(whi, n % RING, j), chunk(wlo, n % RING, j)
                ins = three_passes([bank[:, 2 * j + h, 0:HALF] for h in halves],
                                   [[(wh[:, k, :], wl[:, k, :], x3hi[:, k, half(h)], x3lo[:, k, half(h)])
                                     for k in range(KB)] for h in halves])
                if halves[-1] == 1:
                    ins.then_inc((g_done, u_done)[j], 1)

            def expert_down(e, n, first=False):
                at(pe, h_split, 8 * e + n + 1)
                if n == 0:
                    at(pe, y_out, KB * e)
                wh, wl = chunk(whi, n % RING, 2), chunk(wlo, n % RING, 2)
                for m in range(KB):
                    if first and m == 1:
                        pe.wait_ge(cwT_ready, 1)
                    ms = slice(m * P, (m + 1) * P)
                    for h in range(2):
                        for i, (w, a) in enumerate(((wh, hhi), (wh, hlo), (wl, hhi))):
                            ins = mm(bank[:, 4 + 2 * m + h, 0:HALF], w[:, ms], a[:, n % 2, half(h)],
                                     start=n == 0 and i == 0, stop=n == NF - 1 and i == 2)
                ins.then_inc(chunk_used, 1)

            def expert(e):
                for n in range(NF):
                    gate_up(e, n, 0)
                    gate_up(e, n, 1)
                    if n:
                        expert_down(e, n - 1)
                expert_down(e, NF - 1)

            pe.wait_ge(in_router, 16)
            pe.wait_ge(turned_out, 7)
            gates(0)
            pe.wait_ge(x3_split, 1)
            gate_up(0, 0, 0, (0,))
            gate_up(0, 0, 1, (0,))
            pe.wait_ge(norm_ready, 7)
            turn(7, x3, 1, range(BH - 1, BH))
            pe.wait_ge(turned_out, 8)
            gates(1)
            pe.wait_ge(x3_split, 2)
            gate_up(0, 0, 0, (1,))
            gate_up(0, 0, 1, (1,))
            for n in range(1, NF):
                gate_up(0, n, 0)
                gate_up(0, n, 1)
                if n == 1:
                    pe.wait_ge(cw_ready, 1)
                    for b in range(B):
                        ins = pe.transpose(bank[0:E, 6 + b // BH, (b % BH) * S:(b % BH + 1) * S],
                                           cw[:, b, :], ident[0:S, 0:S])
                    ins.then_inc(cwT_done, 1)
                expert_down(0, n - 1, n == 1)
            expert_down(0, NF - 1)
            with pe.Fori(1, E) as e:
                expert(e)
            for n in range(4):
                for m in range(KB):
                    at(pe, acc_done, KB * (E - 1) + m + 1)
                    for b in range(2):
                        ins = pe.transpose(bank[0:S, n, b * D + m * P:b * D + (m + 1) * P],
                                           acc[:, m, seq(2 * n + b)], ident)
                ins.then_inc(fin_done, 1)


def kernel(**inputs):
    import numpy as np
    import concourse.bacc as bacc
    from concourse.bass_utils import run_bass_kernel_spmd

    def get(name):
        return np.asarray(inputs[name])

    def block1(name):
        return get("L0_attn_" + name)

    def in_blocks(w):
        return w.reshape(-1, P, w.shape[1]).transpose(1, 0, 2)

    square = np.stack([in_blocks(w.T) for w in (
        block1("Wa_w"), block1("Wb_w"), block1("Wo_w"), block1("C_w"), block1("p_w"),
        get("L0_xattn_Wq"), get("L0_xattn_Wk"), get("L0_xattn_Wv"))], axis=1)
    columns = np.concatenate([v.reshape(-1, P).T for v in (
        block1("Wa_b"), block1("Wb_b"), get("L0_xattn_bq"), get("L0_xattn_bk"), block1("f1_b"), block1("f2_b"))], axis=1)
    rows = np.stack([block1("C_b"), block1("Wo_b"), np.repeat(block1("head_weights"), DH), block1("ln_g"),
                     block1("ln_b"), block1("p_b"), get("L0_xattn_bv")])
    heads = np.arange(P)[:, None] // DH % HG == np.arange(HG)[None, :]
    maxima = (np.arange(P)[:, None] < S) | (np.arange(P)[:, None] - S == np.arange(HH)[None, :])
    arrays = {
        "x": get("x").transpose(1, 0, 2),
        "context": get("ctx_1024").transpose(0, 2, 1).reshape(B, KB, P, SK).transpose(0, 2, 1, 3),
        "mask": get("mask_Bx1xSxS2_ik1").reshape(B, S, SK),
        "square": square,
        "ff1": in_blocks(block1("f1_w").T),
        "ff2": in_blocks(block1("f2_w").T),
        "columns": columns,
        "rows": rows,
        "router": np.concatenate([in_blocks(get("L0_ffn_w_router")), in_blocks(get("L0_ffn_w_gating"))], axis=2),
        "gate": get("L0_ffn_w_gate"),
        "up": get("L0_ffn_w_up"),
        "down": get("L0_ffn_w_down"),
        "constants": np.concatenate([np.eye(P), heads, maxima], axis=1).astype(np.float32),
    }
    arrays = {n: np.ascontiguousarray(a) for n, a in arrays.items()}
    nc = bacc.Bacc("TRN2", target_bir_lowering=False, num_devices=1)
    args = [nc.dram_tensor(n, a.shape, mybir.dt.from_np(a.dtype), kind="ExternalInput").ap() for n, a in arrays.items()]
    y = nc.dram_tensor("y", (B, S, D), F32, kind="ExternalOutput").ap()
    decoder_layer(nc, *args, y)
    got = run_bass_kernel_spmd(nc, [arrays], core_ids=[0])
    return got.results[0]["y"]
```

```python
import concourse.bass as bass
from concourse import mybir
from contextlib import ExitStack

F32 = mybir.dt.float32
F32R = mybir.dt.float32r
I32 = mybir.dt.int32
ALU = mybir.AluOpType
ACT = mybir.ActivationFunctionType
AX = mybir.AxisListType

B, S, D = 8, 112, 256
SK = 375
H, DH = 16, 16
P = 128
KB = D // P
T = B * S
HALF = T // 2
BH = B // 2
FF = 1024
NF = FF // P
E = 8
KT, NK = 125, 3
HH = H // KB
HG = 4
NG = H // HG
GP = HG * DH
MR = S + HH
VW = DH + 1
RING = 4
LEAD = RING - 1
LN_EPS = 1e-5
MASKED = -1e30
W_A, W_B, W_O, W_C, W_P, W_Q, W_K, W_V = range(8)
C_A, C_B, C_Q, C_K, C_F1, C_F2 = 0, 2, 4, 6, 8, 16
R_C, R_O, R_HEAD, R_G, R_B, R_P, R_V = range(7)
GATE_SCALE = 10.0 / (1.0 + 1.4901161193847656e-08)
TB = ((0, 1), (6, 7), (4, 5), (2, 3), (6, 7), (6,), (6,), (0, 1), (7, 1))
ZB, FB, PB = (0, 2), (4, 2), (4, 2)
QB = ((4, 5), (6, 6))
BESIDE = (2 * B * D + 4 * KB * T + BH * D + D + 6 * HALF + NF * D
          - (KB * HH * S + KB * NK * HH * S + 2 * NG * HG * S + 2 * H + H * DH
             + 2 * (SK + 1) + KB * MR + 2 * SK + KB * S + B * D + KB * T))
UNDER_X3 = (2 * B * D + 4 * KB * T + BH * D + D + 6 * HALF + NF * D - BESIDE
            - (E * T + 5 * T + B * 2 * E + 4 * B + B * E + B + T))
LN3_PARTS = (slice(0, BH), slice(BH, B - 1), slice(B - 1, B))
LAG = 2


def decoder_layer(nc, x, context, mask, square, ff1, ff2, columns, rows, router, gate, up, down, constants, out):
    ctx = ExitStack()
    with ctx:
        def sb(name, shape, dt=F32, to=ctx):
            return to.enter_context(nc.sbuf_tensor(name, shape, dt))

        def sem(name):
            return ctx.enter_context(nc.semaphore(name))

        xs = sb("xs", [S, B, D])
        consts = sb("consts", [P, P + HG + HH])
        cols = sb("cols", [P, 18])
        rowv = sb("rowv", [KT, 7, D])
        wsq = sb("wsq", [P, 8, KB, D])
        wrt = sb("wrt", [P, KB, 2 * E])
        stats = sb("stats", [S, 4, B, 6])
        mv = sb("mv", [S, 4, B, 2])
        var = sb("var", [S, 4, B])
        rstd = sb("rstd", [S, 4, B])
        nhalf = sb("nhalf", [S, B])
        raw = sb("raw", [P, 2, 12 * D])
        ffw = ctx.enter_context(ExitStack())
        w1hi = sb("w1hi", [P, 2, KB * FF // 2], F32R, to=ffw)
        w1lo = sb("w1lo", [P, 2, KB * FF // 2], F32R, to=ffw)
        w2hi = sb("w2hi", [P, 2, NF // 2 * D], F32R, to=ffw)
        ffw.close()
        whi = sb("whi", [P, RING, 6 * P], F32R)
        wlo = sb("wlo", [P, RING, 6 * P], F32R)
        qhl = sb("qhl", [P, 2, KB, T], F32R)
        qhi, qlo = qhl[:, 0, :, :], qhl[:, 1, :, :]
        wkhi, wklo = (w[:, RING - 2, 0:KB * D].rearrange("p (k f) -> p k f", k=KB) for w in (whi, wlo))
        cxhi, cxlo = (w[:, RING - 1, 0:KB * (SK + 1)].rearrange("p (k t) -> p k t", k=KB) for w in (whi, wlo))
        ident = consts[:, 0:P]
        headmask = consts[:, P:P + HG]
        rowmask = consts[:, P + HG:P + HG + HH]
        cw_dram = nc.dram_tensor("cw_dram", (E, T), F32, kind="Internal").ap()
        bank = ctx.enter_context(nc.psum_tensor("bank", [P, 8, 512], F32))

        one = ctx.enter_context(ExitStack())
        zt = sb("zt", [S, B, D], to=one)
        xn = sb("xn", [S, B, D], to=one)
        nT = sb("nT", [P, KB, T], to=one)
        aT = sb("aT", [P, KB, T], to=one)
        bT = sb("bT", [P, KB, T], to=one)
        hT = sb("hT", [P, KB, T], to=one)
        uT = aT
        uhi, ulo = qhi, qlo
        zb = sb("zb", [S, BH, D], to=one)
        bsum = sb("bsum", [S, D], to=one)
        fT = sb("fT", [P, 2, HALF], to=one)
        fhi = sb("fhi", [P, 2, HALF], F32R, to=one)
        flo = sb("flo", [P, 2, HALF], F32R, to=one)
        w2lo = sb("w2lo", [P, 2, NF // 2 * D], F32R, to=one)
        one.close()

        two = ctx.enter_context(ExitStack())
        weighed = sb("weighed", [MR, KB, HH, S], F32R, to=two)
        prob = sb("prob", [KT, KB, NK, HH * S], to=two)
        qb = [[], []]
        for part in ("high", "low"):
            qb[1].append(sb(f"qb1_{part}", [P, NG, HG, S], F32R, to=two))
        osum = sb("osum", [S, H], to=two)
        orec = sb("orec", [S, H], to=two)
        att = sb("att", [S, H, DH], to=two)
        smaxT = sb("smaxT", [MR, KB, S], to=two)
        mbias = sb("mbias", [MR, 2, SK + 1], F32R, to=two)
        smax = sb("smax", [S, KB, MR], to=two)
        scored = sb("scored", [S, 2, SK], to=two)
        x3 = sb("x3", [S, B, D], to=two)
        x3T = sb("x3T", [P, KB, T], to=two)
        x1n, qf = (xn, x3), (bT, x3T)
        x1T = (nT[:, :, 0:HALF], x3T[:, :, 0:HALF])
        sb("beside", [P, BESIDE], to=two)
        for part in ("high", "low"):
            qb[0].append(sb(f"qb0_{part}", [P, NG, HG, S], F32R, to=two))
        cxt = sb("cxt", [P, 2, KB, SK], to=two)
        keys = sb("keys", [P, 2, NG, SK + 1], F32R, to=two)
        qboth = sb("qboth", [P, 2, NG, S], to=two)
        vs = sb("vs", [KT, 2, NK, H, VW], to=two)
        mask_in = sb("mask_in", [S, 2, SK], I32, to=two)
        some = sb("some", [S, 2, 1], to=two)
        two.close()

        three = ctx.enter_context(ExitStack())
        x3hi, x3lo = qhi, qlo
        cwb = sb("cwb", [P, E, T], to=three)
        sg = sb("sg", [P, 2, T], to=three)
        hid = sb("hid", [P, T], to=three)
        hhi = sb("hhi", [P, 2, T], F32R, to=three)
        lg = sb("lg", [S, B, 2, E], to=three)
        lmax = sb("lmax", [S, B, 2], to=three)
        lsum = sb("lsum", [S, B, 2], to=three)
        cw = sb("cw", [S, B, E], to=three)
        cws = sb("cws", [S, B], to=three)
        cwT = sb("cwT", [E, T], to=three)
        sb("under_x3", [P, UNDER_X3], to=three)
        hlo = sb("hlo", [P, 2, T], F32R, to=three)
        yw = sb("yw", [P, KB, T], to=three)
        acc = sb("acc", [P, KB, T], to=three)
        three.close()

        in_x = [sem(f"in_x{n}") for n in range(2)]
        in_consts, in_rows, in_ab, in_oc, in_pq, in_kv, in_router = map(
            sem, ("in_consts", "in_rows", "in_ab", "in_oc", "in_pq", "in_kv", "in_router"))
        in_ff = [sem(f"in_ff{n}") for n in range(2)]
        in_ctx = [sem(f"in_ctx{n}") for n in range(2)]
        in_mask = [sem(f"in_mask{n}") for n in range(2)]
        in_w = [sem(f"in_w{n}") for n in range(2)]
        out_cw, in_cw, out_done = sem("out_cw"), sem("in_cw"), sem("out_done")
        var_ready, rstd_ready, norm_ready = sem("var_ready"), sem("rstd_ready"), sem("norm_ready")
        dve_step = sem("dve_step")
        pool_step = sem("pool_step")
        turned, turned_out = sem("turned"), sem("turned_out")
        ab_done, a_ready, b_ready, h_ready = sem("ab_done"), sem("a_ready"), sem("b_ready"), sem("h_ready")
        z_done, z_ready, zb_ready, u_ready = sem("z_done"), sem("z_ready"), sem("zb_ready"), sem("u_ready")
        ffw_hi, ffw_lo, u_split = sem("ffw_hi"), sem("ffw_lo"), sem("u_split")
        fhi_ready, last_f_split = sem("fhi_ready"), sem("last_f_split")
        f1_done, gelu_ready, f_split, f2_done, v_ready = (
            sem("f1_done"), sem("gelu_ready"), sem("f_split"), sem("f2_done"), sem("v_ready"))
        p_done, x1_ready, q_done, q_float, q_ready = (
            sem("p_done"), sem("x1_ready"), sem("q_done"), sem("q_float"), sem("q_ready"))
        kv_done, khi_ready, kv_out, mb_ready, mb_some = (
            sem("kv_done"), sem("khi_ready"), sem("kv_out"), sem("mb_ready"), sem("mb_some"))
        qboth_ready, qb_ready, s_done, max_ready = (
            sem("qboth_ready"), sem("qb_ready"), sem("s_done"), sem("max_ready"))
        maxT_done, maxT_out, weighed_ready = sem("maxT_done"), sem("maxT_out"), sem("weighed_ready")
        st_done, exp_done, pv_done, o_out, o_step = (
            sem("st_done"), sem("exp_done"), sem("pv_done"), sem("o_out"), sem("o_step"))
        att_consts, wk_ready, ctx_high, ctx_ready = map(sem, ("att_consts", "wk_ready", "ctx_high", "ctx_ready"))
        passed = sem("passed")
        x3_float, x3_split, lg_done, soft_exp, lg_ready, cw_ready, cwT_done, cwT_ready = map(
            sem, ("x3_float", "x3_split", "lg_done", "soft_exp", "lg_ready", "cw_ready", "cwT_done", "cwT_ready"))
        w_hi, w_lo, g_done, u_done, silu_ready, h_float, hhi_ready, h_split = map(
            sem, ("w_hi", "w_lo", "g_done", "u_done", "silu_ready", "h_float", "hhi_ready", "h_split"))
        chunk_used, y_out, acc_done, fin_done, fin_out = map(
            sem, ("chunk_used", "y_out", "acc_done", "fin_done", "fin_out"))
        last_done, last_out, last_added0, last_added1 = map(
            sem, ("last_done", "last_out", "last_added0", "last_added1"))

        START = ((st_done, 4), (kv_out, 1), (max_ready, 2), (exp_done, 2), (pv_done, 2), (o_out, 1),
                 (maxT_done, 1), (maxT_out, 2), (weighed_ready, 4), (chunk_used, RING), (silu_ready, 1), (h_float, 2), (h_split, 1),
                 (y_out, 1), (acc_done, 3))

        def started(s):
            return sum(n for other, n in START if other is s)

        def at(eng, s, count):
            eng.wait_ge(s, count + started(s))

        def at_all(eng, *counts):
            for s, n in counts:
                at(eng, s, n)
                eng.sem_inc(passed, 1)

        def begin(eng, *sems):
            for s in sems:
                eng.sem_inc(s, started(s))

        def half(b):
            return slice(b * HALF, (b + 1) * HALF)

        def seq(b):
            return slice(b * S, (b + 1) * S)

        def pair(n):
            return bank[:, n:n + 2, 0:HALF]

        gate_v = gate.rearrange("e (k p) f -> e p k f", p=P)
        up_v = up.rearrange("e (k p) f -> e p k f", p=P)
        down_v = down.rearrange("e (n p) d -> e p n d", p=P)

        def raw_part(slot, what):
            if what < 2:
                return raw[:, slot, what * 4 * D:(what + 1) * 4 * D].rearrange("p (k f) -> p k f", k=KB)
            return raw[:, slot, 8 * D:12 * D].rearrange("p (n d) -> p n d", n=4)

        def raw_chunk(slot, n, what):
            if what < 2:
                return raw_part(slot, what)[:, :, n * P:(n + 1) * P]
            return raw_part(slot, 2)[:, n, :]

        def chunk(w, r, what):
            part = w[:, r, what * 2 * P:(what + 1) * 2 * P]
            return part.rearrange("p (k f) -> p k f", k=KB) if what < 2 else part

        block = ctx.enter_context(nc.Block())

        @block.sync
        def _(sp):
            xv = x.rearrange("s (n b) d -> n s b d", n=2)
            sp.dma_start(xs[:, 0:BH, :], xv[0]).then_inc(in_x[0], 16)
            sp.dma_start(consts[:, :], constants).then_inc(in_consts, 16)
            sp.dma_start(cols[:, :], columns).then_inc(in_consts, 16)
            sp.dma_start(xs[:, BH:B, :], xv[1]).then_inc(in_x[1], 16)
            sp.dma_start(wsq[:, W_A:W_B + 1, :, :], square[:, W_A:W_B + 1, :, :]).then_inc(in_ab, 16)
            sp.dma_start(wsq[:, W_O:W_C + 1, :, :], square[:, W_O:W_C + 1, :, :]).then_inc(in_oc, 16)
            sp.dma_start(rowv[:, :, :], rows.rearrange("r d -> (r d)").partition_broadcast(KT)
                         .rearrange("s (r d) -> s r d", r=7)).then_inc(in_rows, 16)
            sp.dma_start(raw[:, 0, 0:KB * FF], ff1.rearrange("p k f -> p (k f)")).then_inc(in_ff[0], 16)
            sp.dma_start(raw[:, 1, 0:NF * D], ff2.rearrange("p n d -> p (n d)")).then_inc(in_ff[1], 16)
            sp.dma_start(wsq[:, W_K:W_V + 1, :, :], square[:, W_K:W_V + 1, :, :]).then_inc(in_kv, 16)

            def load_experts(e, s):
                f = slice(s * FF // 2, (s + 1) * FF // 2)
                n = slice(s * NF // 2, (s + 1) * NF // 2)
                sp.dma_start(raw_part(s, 0), gate_v[e, :, :, f]).then_inc(in_w[s], 16)
                sp.dma_start(raw_part(s, 1), up_v[e, :, :, f]).then_inc(in_w[s], 16)
                sp.dma_start(raw_part(s, 2), down_v[e, :, n, :]).then_inc(in_w[s], 16)

            def load_batch(b, s):
                sp.dma_start(cxt[:, s, :, :], context[b]).then_inc(in_ctx[s], 16)
                sp.dma_start(mask_in[:, s, :], mask[b]).then_inc(in_mask[s], 16)

            load_batch(0, 0)
            sp.dma_start(wsq[:, W_P:W_Q + 1, :, :], square[:, W_P:W_Q + 1, :, :]).then_inc(in_pq, 16)
            load_batch(1, 1)
            sp.dma_start(wrt[:, :, :], router).then_inc(in_router, 16)
            sp.wait_ge(ffw_hi, 4)
            sp.wait_ge(ffw_lo, 4)
            load_experts(0, 0)
            load_experts(0, 1)
            with sp.Fori(0, 3) as i:
                for s in range(2):
                    at_all(sp, (kv_done, 5 * (2 * i + s) + 5), (mb_ready, 2 * i + s + 1))
                    load_batch(2 * i + 2 + s, s)
            sp.wait_ge(cwT_ready, 1)
            sp.dma_start(cw_dram, cwT[:, :]).then_inc(out_cw, 16)
            sp.wait_ge(out_cw, 16)
            sp.dma_start(cwb[:, :, :].rearrange("p e t -> p (e t)"),
                         cw_dram.rearrange("e t -> (e t)").partition_broadcast(P)).then_inc(in_cw, 16)
            with sp.Fori(1, E) as e:
                for s in range(2):
                    at_all(sp, (w_hi, 8 * (e - 1) + 4 * s + 4), (w_lo, 8 * (e - 1) + 4 * s + 4))
                    load_experts(e, s)
            ov = out.rearrange("b s d -> s b d")
            for n in range(4):
                sp.wait_ge(fin_out, n + 1)
                sp.dma_start(ov[:, 2 * n:2 * n + 2, :], xs[:, 2 * n:2 * n + 2, :]).then_inc(out_done, 16)
            sp.wait_ge(out_done, 64)

        @block.gpsimd
        def _(pool):
            count = [0]

            def link(ins):
                count[0] += 1
                ins.then_inc(pool_step, 1)
                pool.wait_ge(pool_step, count[0])

            begin(pool, weighed_ready, acc_done)
            link(pool.memset(nhalf[:, :], -0.5))

            def rsqrt(ln, part, bs=None):
                pool.wait_ge(var_ready, 2 * ln + part + 1)
                bs = bs or slice(part * BH, (part + 1) * BH)
                pool.tensor_tensor(rstd[:, ln, bs], var[:, ln, bs], nhalf[:, bs], ALU.pow).then_inc(rstd_ready, 1)

            rsqrt(0, 0)
            rsqrt(0, 1)
            def weight_low(n, c):
                hi, lo = ((w1hi, w1lo), (w2hi, w2lo))[n]
                pool.wait_ge(ffw_hi, 2 * n + c + 1)
                pool.tensor_tensor(lo[:, c, :], raw[:, n, c * FF:(c + 1) * FF], hi[:, c, :].bitcast(F32),
                                   ALU.subtract).then_inc(ffw_lo, 1)

            def add_ln_b(h):
                pool.wait_ge(z_ready, h + 1)
                if h:
                    pool.wait_ge(u_ready, h)
                pool.tensor_tensor(zb[:, :, :], zt[:, h * BH:(h + 1) * BH, :],
                                   rowv[0:S, R_B, :].unsqueeze(1).to_broadcast([S, BH, D]), ALU.add)\
                    .then_inc(zb_ready, 1)

            def hidden_low(f):
                pool.wait_ge(fhi_ready, f + 1)
                pool.tensor_tensor(flo[:, f % 2, :], fT[:, f % 2, :], fhi[:, f % 2, :].bitcast(F32),
                                   ALU.subtract).then_inc(f_split, 1)

            weight_low(0, 0)
            weight_low(0, 1)
            weight_low(1, 0)
            add_ln_b(0)
            rsqrt(1, 0)
            weight_low(1, 1)
            add_ln_b(1)
            rsqrt(1, 1)
            for f in range(2 * NF - 1):
                hidden_low(f)
                if f == NF + 2:
                    rsqrt(2, 0)

            def spread(b, s, k):
                pool.wait_ge(qboth_ready, b + 1)
                for part, dst in enumerate(qb[s]):
                    for g in (2 * k, 2 * k + 1):
                        q = qboth[:, part, g, :].unsqueeze(1).to_broadcast([P, HG, S])
                        m = headmask.unsqueeze(2).to_broadcast([P, HG, S])
                        pool.tensor_tensor(dst[:, g, :, :], q, m, ALU.mult).then_inc(qb_ready, 1)

            def weigh_rows(b, k, first=False):
                at(pool, maxT_out, 2 * b + k + 1)
                if not first:
                    at(pool, st_done, 6 * (b - 1) + 3 * (k + 1))
                for i in range(2):
                    heads = slice(i * HG, (i + 1) * HG)
                    v = smaxT[:, k, :].unsqueeze(1).to_broadcast([MR, HG, S])
                    m = rowmask[0:MR, heads].unsqueeze(2).to_broadcast([MR, HG, S])
                    pool.tensor_tensor(weighed[:, k, heads, :], v, m, ALU.mult).then_inc(weighed_ready, 1)

            def split_context(b, s, loads):
                at_all(pool, (in_ctx[s], loads), (kv_done, 5 * (b - 1) + KB))
                pool.tensor_copy(cxhi[:, :, 0:SK], cxt[:, s, :, :]).then_inc(ctx_high, 1)
                pool.wait_ge(ctx_high, b)
                pool.tensor_tensor(cxlo[:, :, 0:SK], cxt[:, s, :, :], cxhi[:, :, 0:SK].bitcast(F32),
                                   ALU.subtract).then_inc(ctx_ready, 1)

            spread(0, 0, 0)
            spread(0, 0, 1)
            pool.wait_ge(f2_done, 2 * NF)
            pool.memset(cxhi[:, :, SK:SK + 1].bitcast(F32), 0.0).then_inc(ctx_ready, 1)
            pool.memset(cxlo[:, :, SK:SK + 1].bitcast(F32), 0.0).then_inc(ctx_ready, 1)
            pool.wait_ge(wk_ready, 1)
            pool.tensor_tensor(wklo, wsq[:, W_K, :, :], wkhi.bitcast(F32), ALU.subtract).then_inc(wk_ready, 1)
            split_context(1, 1, 16)
            weigh_rows(0, 0, True)
            rsqrt(2, 1)

            def attend(b, s, loads=None):
                at(pool, st_done, 6 * (b - 1) + 3)
                spread(b + 1, 1 - s, 0)
                weigh_rows(b, 1)
                at(pool, st_done, 6 * b)
                spread(b + 1, 1 - s, 1)
                if loads is not None:
                    split_context(b + 2, s, loads)
                weigh_rows(b + 1, 0)

            def split_low(e, n):
                at(pool, w_hi, 8 * e + n + 1)
                for what in range(3):
                    ins = pool.tensor_tensor(chunk(wlo, n % RING, what), raw_chunk(n // 4, n % 4, what),
                                             chunk(whi, n % RING, what).bitcast(F32), ALU.subtract)
                ins.then_inc(w_lo, 1)

            with pool.Fori(0, 3) as i:
                for s in range(2):
                    attend(2 * i + s, s, 16 * (i + 2))
            attend(6, 0)
            rsqrt(3, 0)
            weigh_rows(B - 1, 1)
            rsqrt(3, 1, LN3_PARTS[1])
            for n in range(LEAD):
                split_low(0, n)
            rsqrt(3, 2, LN3_PARTS[2])

            def accumulate(e):
                for m in range(KB):
                    at(pool, y_out, KB * e + m + 1)
                    at(pool, acc_done, KB * e + m)
                    pool.tensor_tensor(acc[:, m, :], acc[:, m, :], yw[:, m, :], ALU.add).then_inc(acc_done, 1)

            at(pool, o_out, B)
            link(pool.memset(acc[:, :, :], 0.0))
            for n in range(LEAD, NF):
                split_low(0, n)
            for n in range(LEAD):
                split_low(1, n)

            def expert(e, more):
                for n in range(LEAD, NF):
                    split_low(e, n)
                    if n == LEAD:
                        accumulate(e - 1)
                if more:
                    for n in range(LEAD):
                        split_low(e + 1, n)

            with pool.Fori(1, E - 1) as e:
                expert(e, True)
            expert(E - 1, False)
            at(pool, acc_done, KB * (E - 1))
            for h in range(2):
                pool.wait_ge(last_out, 2 * h + 1)
                pool.tensor_tensor(acc[:, 0, half(h)], acc[:, 0, half(h)], yw[:, 0, half(h)], ALU.add)\
                    .then_inc(last_added0, 1)

        @block.scalar
        def _(act):
            begin(act, exp_done, maxT_out, silu_ready)

            def turn_out(n, dst):
                act.wait_ge(turned, n + 1)
                if len(TB[n]) == 1:
                    ins = act.activation(dst, bank[:, TB[n][0], 0:HALF], ACT.Copy)
                elif TB[n][1] == TB[n][0] + 1:
                    ins = act.activation(dst, pair(TB[n][0]), ACT.Copy)
                else:
                    for k in range(KB):
                        ins = act.activation(dst[:, k, :], bank[:, TB[n][k], 0:HALF], ACT.Copy)
                ins.then_inc(turned_out, 1)

            turn_out(0, nT[:, :, half(0)])
            act.wait_ge(in_consts, 32)
            for h in range(2):
                if h:
                    turn_out(1, nT[:, :, half(1)])
                for m in range(KB):
                    act.wait_ge(ab_done, 4 * h + m + 1)
                    act.activation(aT[:, m, half(h)], bank[:, 2 + m, 0:HALF], ACT.Tanh,
                                   bias=cols[:, C_A + m:C_A + m + 1]).then_inc(a_ready, 1)
            for n, hi in enumerate((w1hi, w2hi)):
                act.wait_ge(in_ff[n], 16)
                for c in range(2):
                    act.activation(hi[:, c, :], raw[:, n, c * FF:(c + 1) * FF], ACT.Copy).then_inc(ffw_hi, 1)

            def key_high(b, s, k, kbank=7):
                act.wait_ge(kv_done, 5 * b + k + 1)
                for i in range(2):
                    own = slice(i * GP, (i + 1) * GP)
                    ins = act.activation(keys[own, s, 2 * k + i, 0:SK], bank[own, kbank, 0:SK], ACT.Identity,
                                         bias=cols[own, C_K + k:C_K + k + 1])
                ins.then_inc(khi_ready, 1)

            key_high(0, 0, 0)
            act.wait_ge(h_ready, 4)
            turn_out(2, uT[:, :, half(0)])
            key_high(0, 0, 1, 6)

            def hidden_high(f):
                n = f % NF
                act.wait_ge(f1_done, f + 1)
                if f >= 2:
                    act.wait_ge(f_split, f - 1)
                act.activation(fT[:, f % 2, :], bank[:, f % 2, 0:HALF], ACT.Gelu,
                               bias=cols[:, C_F1 + n:C_F1 + n + 1]).then_inc(gelu_ready, 1)
                act.wait_ge(gelu_ready, f + 1)
                if f >= 2:
                    act.wait_ge(f2_done, f - 1)
                act.activation(fhi[:, f % 2, :], fT[:, f % 2, :], ACT.Copy).then_inc(fhi_ready, 1)

            def both(b):
                act.wait_ge(qb_ready, 8 * b)
                first_both(b)

            def first_both(b):
                for rows in (slice(0, GP), slice(GP, P)):
                    for i in range(2):
                        own = slice(i * GP, (i + 1) * GP)
                        ins = act.activation(qboth[rows, :, i:NG:2, :],
                                             qhl[own, :, :, bass.ds(b * S, S)].bitcast(F32), ACT.Copy)
                ins.then_inc(qboth_ready, 1)

            for f in range(2 * NF):
                if f == NF + 5:
                    turn_out(4, x1T[0])
                if f == 2 * NF - 1:
                    act.wait_ge(q_ready, 1)
                    first_both(0)
                hidden_high(f)
                if f == 5:
                    turn_out(3, uT[:, :, half(1)])

            def max_out(b, k):
                at(act, maxT_done, 2 * b + k + 1)
                at(act, weighed_ready, 2 * (2 * b + k) - 2)
                act.activation(smaxT[:, k, :], bank[0:MR, 7, 0:S], ACT.Copy)\
                   .then_inc(maxT_out, 1)

            def exps(b, u):
                k, t = u // NK, u % NK
                at(act, st_done, 6 * b + u + 1)
                at(act, pv_done, 2 * b + k - 1)
                act.activation(prob[:, k, t, :].rearrange("p (g t) -> p g t", g=2),
                               bank[0:KT, 2 + 2 * (u % 2):4 + 2 * (u % 2), 0:HG * S], ACT.Exp).then_inc(exp_done, 1)

            act.wait_ge(f2_done, 2 * NF)
            act.activation(wkhi, wsq[:, W_K, :, :], ACT.Copy).then_inc(wk_ready, 1)
            max_out(0, 0)

            def split_high(e, n):
                c = 8 * e + n
                if n % 4 == 0:
                    act.wait_ge(in_w[n // 4], 48 * (e + 1))
                at(act, chunk_used, c + 1 - RING)
                for what in range(3):
                    ins = act.activation(chunk(whi, n % RING, what), raw_chunk(n // 4, n % 4, what), ACT.Copy)
                ins.then_inc(w_hi, 1)

            def attend(b, s, more, first=False):
                if more:
                    key_high(b + 1, 1 - s, 0)
                exps(b, 0)
                if more:
                    both(b + 1)
                exps(b, 1)
                if first:
                    turn_out(5, x1T[1][:, 0, :])
                    turn_out(6, x1T[1][:, 1, :])
                if not more:
                    split_high(0, 0)
                max_out(b, 1)
                exps(b, 2)
                if more:
                    key_high(b + 1, 1 - s, 1)
                exps(b, 3)
                if not more:
                    split_high(0, 1)
                    turn_out(7, x3T[:, :, half(0)])
                exps(b, 4)
                if more:
                    max_out(b + 1, 0)
                else:
                    split_high(0, 2)
                exps(b, 5)

            attend(0, 0, True, True)
            act.wait_ge(q_ready, 2)
            with act.Fori(0, 3) as i:
                for s in (1, 0):
                    attend(2 * i + 2 - s, s, True)
            attend(7, 1, False)

            turn_out(8, x3T[:, :, half(1)])
            def silu(e, n):
                f = 8 * e + n
                act.wait_ge(g_done, f + 1)
                at(act, h_float, f - 1)
                act.activation(sg[:, n % 2, :].rearrange("p (h t) -> p h t", h=2), pair(0), ACT.Silu)\
                   .then_inc(silu_ready, 1)

            silu(0, 0)
            act.wait_ge(lg_ready, 1)
            for j, scale in enumerate((1.0, GATE_SCALE)):
                act.activation(lg[:, :, j, :], lg[:, :, j, :], ACT.Exp, scale=scale).then_inc(soft_exp, 1)
            def weights_out():
                act.wait_ge(cwT_done, 1)
                act.activation(cwT[:, :].rearrange("e (h t) -> e h t", h=2), bank[0:E, 6:8, 0:HALF], ACT.Copy)\
               .then_inc(cwT_ready, 1)

            def expert(e, more, first=False):
                for n in range(NF):
                    if not (first and n == 0):
                        silu(e, n)
                    if first and n == 1:
                        weights_out()
                    if n < NF - LEAD:
                        split_high(e, n + LEAD)
                    elif more:
                        split_high(e + 1, n + LEAD - NF)

            expert(0, True, True)
            with act.Fori(1, E - 1) as e:
                expert(e, True)
            expert(E - 1, False)

        @block.vector
        def _(dve):
            count = [0]

            def did(ins):
                count[0] += 1
                ins.then_inc(dve_step, 1)

            def sync():
                dve.wait_ge(dve_step, count[0])

            begin(dve, kv_out, max_ready, o_out, h_float, h_split, y_out)

            def sequences(h, bs):
                return range(bs.start, bs.stop) if bs else range(h * BH, (h + 1) * BH)

            def statistics(ln, h, src, bs=None):
                bs = sequences(h, bs)
                for b in bs:
                    did(dve.bn_stats(stats[:, ln, b, :], src[:, b, :]))
                sync()
                for b in bs:
                    did(dve.bn_aggr(mv[:, ln, b, :], stats[:, ln, b, :]))
                sync()
                dve.tensor_scalar(var[:, ln, bs.start:bs.stop], mv[:, ln, bs.start:bs.stop, 1], LN_EPS, None,
                                  ALU.add).then_inc(var_ready, 1)

            def normalize(ln, h, src, dst, bs=None):
                dve.wait_ge(rstd_ready, 2 * ln + h + 1)
                for b in sequences(h, bs):
                    did(dve.tensor_scalar(dst[:, b, :], src[:, b, :], mv[:, ln, b, 0:1], rstd[:, ln, b:b + 1],
                                          ALU.subtract, ALU.mult))
                sync()

            for h in range(2):
                dve.wait_ge(in_x[h], 16)
                statistics(0, h, xs)
                normalize(0, h, xs, xn)
                dve.sem_inc(norm_ready, 1)
            dve.wait_ge(in_rows, 16)
            did(dve.tensor_tensor(bsum[:, :], rowv[0:S, R_C, :], rowv[0:S, R_O, :], ALU.add))
            did(dve.tensor_tensor(xs[:, :, :], xs[:, :, :],
                                  rowv[0:S, R_P, :].unsqueeze(1).to_broadcast([S, B, D]), ALU.add))
            dve.wait_ge(in_consts, 32)
            dve.memset(vs[:, :, :, :, DH:VW], 1.0).then_inc(att_consts, 1)
            dve.memset(keys[:, :, :, SK:SK + 1].bitcast(F32), 0.0).then_inc(att_consts, 1)
            for h in range(2):
                for m in range(KB):
                    dve.wait_ge(ab_done, 4 * h + 2 + m + 1)
                    dve.tensor_scalar(bT[:, m, half(h)], bank[:, 4 + m, 0:HALF], cols[:, C_B + m:C_B + m + 1], None,
                                      ALU.add).then_inc(b_ready, 1)
                for m in range(KB):
                    dve.wait_ge(a_ready, 2 * h + m + 1)
                    first = aT[:, m, half(h)].rearrange("p (b t) -> p b t", b=BH)[:, :, 0:1]
                    did(dve.memset(first, 0.0))
                    sync()
                    dve.wait_ge(b_ready, 2 * h + m + 1)
                    dve.tensor_tensor_scan(hT[:, m, half(h)], aT[:, m, half(h)], bT[:, m, half(h)], 0.0,
                                           ALU.mult, ALU.add).then_inc(h_ready, 1)

            def key_low(b, s, k, kbank=7):
                dve.wait_ge(khi_ready, KB * b + k + 1)
                for i in range(2):
                    own, other = slice(i * GP, (i + 1) * GP), slice((1 - i) * GP, (2 - i) * GP)
                    ins = dve.scalar_tensor_tensor(
                        keys[other, s, 2 * k + i, 0:SK], bank[own, kbank, 0:SK], cols[own, C_K + k:C_K + k + 1],
                        keys[own, s, 2 * k + i, 0:SK].bitcast(F32), ALU.add, ALU.subtract)
                ins.then_inc(kv_out, 1)

            def values(b, s, t):
                dve.wait_ge(kv_done, 5 * b + KB + t + 1)
                dve.tensor_tensor(vs[:, s, t, :, 0:DH], bank[0:KT, 7, 0:D].rearrange("t (h d) -> t h d", h=H),
                                  rowv[:, R_V, :].rearrange("t (h d) -> t h d", h=H), ALU.add).then_inc(kv_out, 1)

            def mask_bias(b, s, loads, first=False):
                dve.wait_ge(in_mask[s], loads)
                if not first:
                    at(dve, st_done, 6 * (b - 1))
                dve.tensor_scalar(mbias[0:S, s, 0:SK], mask_in[:, s, :], 0.0, MASKED, ALU.is_equal, ALU.mult)\
                   .then_inc(mb_ready, 1)
                dve.wait_ge(mb_ready, b + 1)
                dve.tensor_reduce(some[:, s, :], mbias[0:S, s, 0:SK].bitcast(F32), AX.X, ALU.max).then_inc(mb_some, 1)
                dve.wait_ge(mb_some, 2 * b + 1)
                dve.tensor_scalar(some[:, s, :], some[:, s, :], -1.0, None, ALU.is_ge).then_inc(mb_some, 1)

            def z_of(h):
                for n in range(2):
                    dve.wait_ge(z_done, 2 * h + n + 1)
                    zs = slice(h * BH + 2 * n, h * BH + 2 * n + 2)
                    did(dve.tensor_tensor(zt[:, zs, :], bank[0:S, ZB[h] + n, :].rearrange("s (b d) -> s b d", b=2),
                                          bsum[:, :].unsqueeze(1).to_broadcast([S, 2, D]), ALU.add))
                sync()
                bs = slice(h * BH, (h + 1) * BH)
                did(dve.tensor_tensor(zt[:, bs, :], zt[:, bs, :],
                                      rowv[0:S, R_HEAD, :].unsqueeze(1).to_broadcast([S, BH, D]), ALU.mult))
                sync()
                dve.sem_inc(z_ready, 1)

            def u_of(h):
                statistics(1, h, zt)
                for b in range(h * BH, (h + 1) * BH):
                    did(dve.scalar_tensor_tensor(xn[:, b, :], zt[:, b, :], mv[:, 1, b, 0:1], rowv[0:S, R_G, :],
                                                 ALU.subtract, ALU.mult))
                sync()
                dve.wait_ge(rstd_ready, 2 + h + 1)
                dve.wait_ge(zb_ready, h + 1)
                for b in range(h * BH, (h + 1) * BH):
                    ins = dve.scalar_tensor_tensor(xn[:, b, :], xn[:, b, :], rstd[:, 1, b:b + 1],
                                                   zb[:, b - h * BH, :], ALU.mult, ALU.add)
                ins.then_inc(u_ready, 1)

            def split_u(h):
                dve.wait_ge(turned_out, 2 + h + 1)
                did(dve.tensor_copy(uhi[:, :, half(h)], uT[:, :, half(h)]))
                sync()
                dve.tensor_tensor(ulo[:, :, half(h)], uT[:, :, half(h)], uhi[:, :, half(h)].bitcast(F32),
                                  ALU.subtract).then_inc(u_split, 1)

            def v_of(h):
                dve.wait_ge(f2_done, NF * (h + 1))
                for m in range(KB):
                    dve.scalar_tensor_tensor(hT[:, m, half(h)], bank[:, FB[h] + m, 0:HALF],
                                             cols[:, C_F2 + m:C_F2 + m + 1], uT[:, m, half(h)],
                                             ALU.add, ALU.add).then_inc(v_ready, 1)

            def add_p(h, n):
                dve.wait_ge(p_done, 2 * h + n + 1)
                xb = slice(h * BH + 2 * n, h * BH + 2 * n + 2)
                did(dve.tensor_tensor(xs[:, xb, :], bank[0:S, PB[h] + n, :].rearrange("s (b d) -> s b d", b=2),
                                      xs[:, xb, :], ALU.add))

            def ln2(h):
                normalize(2, h, xs, x1n[h])
                dve.sem_inc(norm_ready, 1)

            def query(h, m):
                dve.wait_ge(q_done, 2 * h + m + 1)
                dve.tensor_scalar(qf[h][:, m, half(h)], bank[:, QB[h][m], 0:HALF], cols[:, C_Q + m:C_Q + m + 1],
                                  float(DH) ** -0.5, ALU.add, ALU.mult).then_inc(q_float, 1)

            def split_q(h):
                dve.wait_ge(q_float, 2 * h + 2)
                did(dve.tensor_copy(qhi[:, :, half(h)], qf[h][:, :, half(h)]))
                sync()
                dve.tensor_tensor(qlo[:, :, half(h)], qf[h][:, :, half(h)], qhi[:, :, half(h)].bitcast(F32),
                                  ALU.subtract).then_inc(q_ready, 1)

            z_of(0)
            u_of(0)
            z_of(1)
            split_u(0)
            u_of(1)
            key_low(0, 0, 0)
            key_low(0, 0, 1, 6)
            for t in range(NK):
                values(0, 0, t)
            split_u(1)
            dve.tensor_copy(smax[:, :, 0:S], ident[0:S, 0:S].unsqueeze(1).to_broadcast([S, KB, S]))\
               .then_inc(att_consts, 1)
            dve.memset(mbias[96:MR, :, :].bitcast(F32), -1.0).then_inc(att_consts, 1)
            dve.wait_ge(att_consts, 4)
            mask_bias(0, 0, 16, True)
            v_of(0)
            add_p(0, 0)
            add_p(0, 1)
            sync()
            statistics(2, 0, xs)
            ln2(0)
            query(0, 0)
            query(0, 1)
            split_q(0)

            def row_max(b, s, h):
                at_all(dve, (s_done, H * b + h + 2), (max_ready, H * b + h),
                       *([(maxT_done, 2 * (b - 1) + h // HH + 1)] if h % HH == 0 else []))
                for i in range(2):
                    dve.tensor_tensor_reduce(out=scored[:, i, :], in0=bank[0:S, i, 0:SK],
                                             in1=mbias[0:S, s, 0:SK].bitcast(F32), scale=1.0, scalar=3 * MASKED,
                                             op0=ALU.add, op1=ALU.max,
                                             accum_out=smax[:, h // HH, S + h % HH + i:S + h % HH + i + 1])\
                       .then_inc(max_ready, 1)

            def output(b, s):
                at(dve, pv_done, 2 * b + 2)
                o = bank[0:S, 6, 0:H * VW].rearrange("s (h v) -> s h v", h=H)
                dve.reciprocal(orec[:, :], o[:, :, DH]).then_inc(o_step, 1)
                dve.wait_ge(o_step, 3 * b + 1)
                dve.tensor_scalar(osum[:, :], orec[:, :], some[:, s, :], None, ALU.mult).then_inc(o_step, 1)
                dve.wait_ge(o_step, 3 * b + 2)
                dve.tensor_tensor(att[:, :, :], o[:, :, 0:DH], osum[:, :].unsqueeze(2).to_broadcast([S, H, DH]),
                                  ALU.mult).then_inc(o_step, 1)
                dve.wait_ge(o_step, 3 * b + 3)
                xb = xs[:, bass.ds(b, 1), :].rearrange("s o d -> s (o d)")
                dve.tensor_tensor(xb, xb, att[:, :, :].rearrange("s h d -> s (h d)"), ALU.add).then_inc(o_out, 1)

            dve.wait_ge(fhi_ready, 2 * NF)
            dve.tensor_tensor(flo[:, 1, :], fT[:, 1, :], fhi[:, 1, :].bitcast(F32), ALU.subtract)\
               .then_inc(last_f_split, 1)
            v_of(1)
            row_max(0, 0, 0)
            add_p(1, 0)
            row_max(0, 0, 2)
            row_max(0, 0, 4)
            add_p(1, 1)
            row_max(0, 0, 6)
            sync()
            statistics(2, 1, xs)

            def attend(b, s, before, loads, first=False):
                key_low(b + 1, 1 - s, 0)
                for h in (8, 10, 12, 14):
                    row_max(b, s, h)
                    if first and h == 8:
                        ln2(1)
                if before:
                    output(b - 1, 1 - s)
                mask_bias(b + 1, 1 - s, loads)
                key_low(b + 1, 1 - s, 1)
                if first:
                    query(1, 0)
                row_max(b + 1, 1 - s, 0)
                if first:
                    query(1, 1)
                values(b + 1, 1 - s, 0)
                row_max(b + 1, 1 - s, 2)
                row_max(b + 1, 1 - s, 4)
                values(b + 1, 1 - s, 1)
                row_max(b + 1, 1 - s, 6)
                values(b + 1, 1 - s, 2)

            attend(0, 0, False, 16, True)
            split_q(1)
            with dve.Fori(0, 3) as i:
                for s in (1, 0):
                    b = 2 * i + 1 if s else 2 * i + 2
                    attend(b, s, True, 16 * (i + 2))
            def ln3(part):
                normalize(3, part, xs, x3, LN3_PARTS[part])
                dve.sem_inc(norm_ready, 1)

            def split_x3(h):
                dve.wait_ge(turned_out, 7 + h + 1)
                did(dve.tensor_copy(x3hi[:, :, half(h)], x3T[:, :, half(h)]))
                sync()
                dve.tensor_tensor(x3lo[:, :, half(h)], x3T[:, :, half(h)], x3hi[:, :, half(h)].bitcast(F32),
                                  ALU.subtract).then_inc(x3_split, 1)

            at(dve, o_out, BH)
            statistics(3, 0, xs, LN3_PARTS[0])
            for h in range(HH, H, 2):
                row_max(B - 1, 1, h)
            ln3(0)
            output(B - 2, 0)
            at(dve, o_out, B - 1)
            statistics(3, 1, xs, LN3_PARTS[1])
            ln3(1)
            dve.wait_ge(qboth_ready, B)
            split_x3(0)
            output(B - 1, 1)
            at(dve, o_out, B)
            statistics(3, 2, xs, LN3_PARTS[2])
            ln3(2)
            split_x3(1)

            def hidden(e, n):
                f = 8 * e + n
                at(dve, silu_ready, f + 1)
                dve.wait_ge(u_done, f + 1)
                at(dve, h_split, f)
                dve.tensor_tensor(hid[:, :].rearrange("p (h t) -> p h t", h=2), pair(2),
                                  sg[:, n % 2, :].rearrange("p (h t) -> p h t", h=2), ALU.mult).then_inc(h_float, 1)
                at(dve, h_float, f + 1)
                at(dve, chunk_used, f - 1)
                dve.tensor_copy(hhi[:, n % 2, :], hid[:, :]).then_inc(hhi_ready, 1)
                dve.wait_ge(hhi_ready, f + 1)
                dve.tensor_tensor(hlo[:, n % 2, :], hid[:, :], hhi[:, n % 2, :].bitcast(F32),
                                  ALU.subtract).then_inc(h_split, 1)

            hidden(0, 0)
            dve.wait_ge(lg_done, 1)
            logits = bank[0:S, 4, 0:B * 2 * E].rearrange("s (b j e) -> s b j e", b=B, j=2)
            did(dve.tensor_reduce(lmax[:, :, :], logits, AX.X, ALU.max))
            sync()
            dve.tensor_tensor(lg[:, :, :, :].rearrange("s b j e -> s (b j) e"), logits.rearrange("s b j e -> s (b j) e"),
                              lmax[:, :, :].rearrange("s b j -> s (b j)").unsqueeze(2).to_broadcast([S, 2 * B, E]),
                              ALU.subtract).then_inc(lg_ready, 1)
            dve.wait_ge(soft_exp, 2)
            did(dve.tensor_reduce(lsum[:, :, :], lg[:, :, :, :], AX.X, ALU.add))
            sync()
            did(dve.reciprocal(lsum[:, :, :], lsum[:, :, :]))
            sync()
            did(dve.tensor_tensor(lg[:, :, :, :].rearrange("s b j e -> s (b j) e"),
                                  lg[:, :, :, :].rearrange("s b j e -> s (b j) e"),
                                  lsum[:, :, :].rearrange("s b j -> s (b j)").unsqueeze(2).to_broadcast([S, 2 * B, E]),
                                  ALU.mult))
            sync()
            did(dve.tensor_tensor(cw[:, :, :], lg[:, :, 0, :], lg[:, :, 1, :], ALU.mult))
            sync()
            did(dve.tensor_reduce(cws[:, :], cw[:, :, :], AX.X, ALU.add))
            sync()
            did(dve.tensor_scalar(cws[:, :], cws[:, :], 1e-9, None, ALU.add))
            sync()
            did(dve.reciprocal(cws[:, :], cws[:, :]))
            sync()
            dve.tensor_tensor(cw[:, :, :], cw[:, :, :], cws[:, :].unsqueeze(2).to_broadcast([S, B, E]),
                              ALU.mult).then_inc(cw_ready, 1)

            def weigh(e):
                at(dve, chunk_used, 8 * e + 8)
                for m in range(KB):
                    at(dve, acc_done, KB * (e - 1) + m + 1)
                    dve.tensor_tensor(yw[:, m, :].rearrange("p (h t) -> p h t", h=2), pair(4 + 2 * m),
                                      cwb[:, bass.ds(e, 1), :].rearrange("p o (h t) -> p (o h) t", h=2),
                                      ALU.mult).then_inc(y_out, 1)

            for n in range(1, NF):
                hidden(0, n)
            dve.wait_ge(in_cw, 16)
            with dve.Fori(1, E) as e:
                hidden(e, 0)
                weigh(e - 1)
                for n in range(1, NF):
                    hidden(e, n)
            for h in range(2):
                dve.wait_ge(last_done, h + 1)
                for m in range(KB):
                    at(dve, acc_done, KB * (E - 2) + m + 1)
                    dve.tensor_tensor(yw[:, m, half(h)], bank[:, 4 + 2 * m + h, 0:HALF],
                                      cwb[:, E - 1, half(h)], ALU.mult).then_inc(last_out, 1)
                dve.wait_ge(last_out, 2 * h + 2)
                dve.tensor_tensor(acc[:, 1, half(h)], acc[:, 1, half(h)], yw[:, 1, half(h)], ALU.add)\
                   .then_inc(last_added1, 1)
            for n in range(4):
                dve.wait_ge(fin_done, n + 1)
                dve.tensor_tensor(xs[:, 2 * n:2 * n + 2, :], bank[0:S, n, :].rearrange("s (b d) -> s b d", b=2),
                                  xs[:, 2 * n:2 * n + 2, :], ALU.add).then_inc(fin_out, 1)

        @block.tensor
        def _(pe):
            begin(pe, st_done, pv_done, maxT_done, chunk_used)
            mm = pe.matmul

            def turn(n, src, h, some=range(BH), ks=range(KB)):
                for k in ks:
                    for b in some:
                        ins = pe.transpose(bank[:, TB[n][k - ks[0]], b * S:(b + 1) * S],
                                           src[:, h * BH + b, k * P:(k + 1) * P], ident[0:S, 0:S])
                if some[-1] == BH - 1:
                    ins.then_inc(turned, 1)

            pe.wait_ge(in_consts, 32)
            pe.wait_ge(norm_ready, 1)
            turn(0, xn, 0)
            pe.wait_ge(in_ab, 16)
            for h in range(2):
                pe.wait_ge(turned_out, h + 1)
                for j, w in enumerate((W_A, W_B)):
                    for m in range(KB):
                        if h:
                            pe.wait_ge((a_ready, b_ready)[j], m + 1)
                        for k in range(KB):
                            ins = mm(bank[:, 2 + 2 * j + m, 0:HALF], wsq[:, w, k, m * P:(m + 1) * P],
                                     nT[:, k, half(h)], start=k == 0, stop=k == KB - 1)
                        ins.then_inc(ab_done, 1)
                    if (h, j) == (0, 0):
                        pe.wait_ge(norm_ready, 2)
                        turn(1, xn, 1)
            pe.wait_ge(in_oc, 16)
            for h in range(2):
                pe.wait_ge(h_ready, 2 * h + 2)
                pe.wait_ge(turned_out, 2)
                for b in range(BH):
                    o = bank[0:S, ZB[h] + b // 2, (b % 2) * D:(b % 2 + 1) * D]
                    for n, (src, w) in enumerate(((nT, W_O), (hT, W_C))):
                        for k in range(KB):
                            ins = mm(o, src[:, k, seq(h * BH + b)], wsq[:, w, k, :],
                                     start=(n, k) == (0, 0), stop=(n, k) == (1, KB - 1))
                    if b % 2:
                        ins.then_inc(z_done, 1)
            def three_passes(outs, pairs):
                for o, ps in zip(outs, pairs):
                    n = 3 * len(ps)
                    i = 0
                    for whi_, wlo_, mhi, mlo in ps:
                        for w, m in ((whi_, mhi), (whi_, mlo), (wlo_, mhi)):
                            last = mm(o, w, m, start=i == 0, stop=i == n - 1)
                            i += 1
                return last

            def ff_up(f):
                h, n = divmod(f, NF)
                if f >= 2:
                    pe.wait_ge(gelu_ready, f - 1)
                w = slice(n * P, (n + 1) * P)
                three_passes([bank[:, f % 2, 0:HALF]],
                             [[(w1hi[:, k, w], w1lo[:, k, w], uhi[:, k, half(h)], ulo[:, k, half(h)])
                               for k in range(KB)]]).then_inc(f1_done, 1)

            def ff_down(f):
                h, n = divmod(f, NF)
                if f < 2 * NF - 1:
                    pe.wait_ge(f_split, f + 1)
                else:
                    pe.wait_ge(last_f_split, 1)
                for m in range(KB):
                    w = slice((n % 4) * D + m * P, (n % 4) * D + (m + 1) * P)
                    for i, (wt, a) in enumerate(((w2hi, fhi), (w2hi, flo), (w2lo, fhi))):
                        ins = mm(bank[:, FB[h] + m, 0:HALF], wt[:, n // 4, w], a[:, f % 2, :],
                                 start=n == 0 and i == 0, stop=n == NF - 1 and i == 2)
                ins.then_inc(f2_done, 1)

            def p_of(h, b):
                o = bank[0:S, PB[h] + b // 2, (b % 2) * D:(b % 2 + 1) * D]
                for k in range(KB):
                    if b == 0:
                        pe.wait_ge(v_ready, 2 * h + k + 1)
                    ins = mm(o, hT[:, k, seq(h * BH + b)], wsq[:, W_P, k, :], start=k == 0, stop=k == KB - 1)
                if b % 2:
                    ins.then_inc(p_done, 1)

            def query(h, m):
                pe.wait_ge(turned_out, 5 + 2 * h)
                if (h, m) == (1, 1):
                    pe.wait_ge(q_float, 3)
                for k in range(KB):
                    ins = mm(bank[:, QB[h][m], 0:HALF], wsq[:, W_Q, k, m * P:(m + 1) * P], x1T[h][:, k, :],
                             start=k == 0, stop=k == KB - 1)
                ins.then_inc(q_done, 1)

            def key_value(b, s, g, loads=None, turned_before=True, kbank=7):
                if loads is not None:
                    pe.wait_ge(in_ctx[s], loads)
                at(pe, kv_out, 5 * b + (g if kbank == 7 else 0))
                if g < KB and turned_before:
                    at(pe, maxT_out, 2 * b + g - 1)
                if g < KB and turned_before:
                    pe.wait_ge(ctx_ready, b + 2)
                    gs = slice(g * P, (g + 1) * P)
                    three_passes([bank[:, 7, 0:SK + 1]],
                                 [[(wkhi[:, k, gs], wklo[:, k, gs], cxhi[:, k, :], cxlo[:, k, :]) for k in range(KB)]])\
                        .then_inc(kv_done, 1)
                    return
                for k in range(KB):
                    c = cxt[:, s, k, :]
                    if g < KB:
                        ins = mm(bank[:, kbank, 0:SK], wsq[:, W_K, k, g * P:(g + 1) * P], c,
                                 start=k == 0, stop=k == KB - 1)
                    else:
                        t = g - KB
                        ins = mm(bank[0:KT, 7, 0:D], c[:, t * KT:(t + 1) * KT], wsq[:, W_V, k, :],
                                 start=k == 0, stop=k == KB - 1)
                ins.then_inc(kv_done, 1)

            pe.wait_ge(in_kv, 16)
            key_value(0, 0, 0, 16, False)
            pe.wait_ge(u_ready, 1)
            turn(2, xn, 0)
            key_value(0, 0, 1, None, False, 6)
            pe.wait_ge(u_split, 1)
            pe.wait_ge(ffw_lo, 4)
            for f in range(2 * NF + LAG):
                if f == NF:
                    pe.wait_ge(u_split, 2)
                if f < 2 * NF:
                    ff_up(f)
                if f == NF + 5:
                    pe.wait_ge(norm_ready, 3)
                    turn(4, xn, 0)
                if f >= LAG:
                    ff_down(f - LAG)
                if f in (3, 4, 5):
                    key_value(0, 0, f - 1, None, False)
                if f == 5:
                    pe.wait_ge(u_ready, 2)
                    turn(3, xn, 1)
                if f == NF + LAG:
                    pe.wait_ge(in_pq, 16)
                    for b in range(BH):
                        p_of(0, b)
                if f == NF + 5:
                    query(0, 0)
                    query(0, 1)

            def score(b, s, h):
                if h % HH == 0:
                    at(pe, kv_out, 5 * b + 1 + h // HH)
                    at(pe, qb_ready, 8 * b + h // HH * 4 + 2)
                at(pe, max_ready, H * b + h - 1)
                g, j = h // HG, h % HG
                mm(bank[0:S, h % 2, 0:SK + 1], qb[s][0][:, g, j, :], keys[:, s, g, :], start=True, stop=True)\
                    .then_inc(s_done, 1)

            def turn_max(b, k, last=False):
                at(pe, max_ready, H * b + HH * (k + 1))
                at(pe, kv_out, 5 * b + 5 + (k == 1 and not last))
                pe.transpose(bank[0:MR, 7, 0:S], smax[:, k, :], ident[0:S, 0:S])\
                  .then_inc(maxT_done, 1)

            def scores_t(b, s, u, i):
                k, t = u // NK, u % NK
                if i == 0:
                    at(pe, exp_done, 6 * b + u - 1)
                    if t == 0:
                        at(pe, qb_ready, 8 * b + 4 * k + 4)
                ks = slice(t * KT, (t + 1) * KT)
                o = bank[0:KT, 2 + 2 * (u % 2) + i, 0:HG * S]
                g = 2 * k + i
                mm(o, keys[:, s, g, ks], qb[s][0][:, g, :, :].rearrange("p h t -> p (h t)"), start=True, stop=False)
                mm(o, keys[:, s, g, ks], qb[s][1][:, g, :, :].rearrange("p h t -> p (h t)"), start=False, stop=False)
                if t == 0:
                    at(pe, weighed_ready, 2 * (2 * b + k) + i + 1)
                ins = mm(o, mbias[:, s, ks],
                         weighed[:, k, i * HG:(i + 1) * HG, :].rearrange("p h t -> p (h t)"), start=False, stop=True)
                if i:
                    ins.then_inc(st_done, 1)

            def weighted(b, s, k, heads):
                if heads[0] == 0:
                    at(pe, exp_done, 6 * b + 3 * k + 3)
                    if k == 0:
                        at(pe, o_out, b)
                        at(pe, kv_out, 5 * b + 5)
                for j in heads:
                    h = k * HH + j
                    for t in range(NK):
                        ins = mm(bank[0:S, 6, h * VW:(h + 1) * VW], prob[:, k, t, j * S:(j + 1) * S],
                                 vs[:, s, t, h, :], start=t == 0, stop=t == NK - 1)
                if heads[-1] == HH - 1:
                    ins.then_inc(pv_done, 1)

            pe.wait_ge(att_consts, 4)
            pe.wait_ge(mb_ready, 1)

            def first_pair(h):
                score(0, 0, h)
                score(0, 0, h + 1)

            first_pair(0)
            p_of(1, 0)
            for b in range(1, BH):
                p_of(1, b)
                first_pair(2 * b)
            turn_max(0, 0)

            def turn_x1(k):
                pe.wait_ge(norm_ready, 4)
                if k:
                    pe.wait_ge(turned_out, 6)
                turn(5 + k, x3, 1, ks=(k,))

            def attend(b, s, before, more, loads):
                def pair(h):
                    score(b, s, h)
                    score(b, s, h + 1)

                def next_pair(h):
                    if more:
                        score(b + 1, 1 - s, h)
                        score(b + 1, 1 - s, h + 1)

                def next_group(g):
                    if more:
                        key_value(b + 1, 1 - s, g, loads if g == 0 else None)

                def former(*heads):
                    if before:
                        weighted(b - 1, 1 - s, 1, heads)
                    elif heads in ((3,), (5,)):
                        turn_x1(heads[0] // 5)

                def now(*heads):
                    weighted(b, s, 0, heads)

                next_group(0)
                scores_t(b, s, 0, 0)
                pair(8)
                scores_t(b, s, 0, 1)
                former(0)
                scores_t(b, s, 1, 0)
                former(1)
                pair(10)
                scores_t(b, s, 1, 1)
                former(2)
                former(3)
                pair(12)
                scores_t(b, s, 2, 0)
                former(4)
                pair(14)
                former(5)
                former(6)
                former(7)
                turn_max(b, 1, not more)
                scores_t(b, s, 2, 1)
                next_group(1)
                if not before:
                    query(1, 0)
                scores_t(b, s, 3, 0)
                next_pair(0)
                scores_t(b, s, 3, 1)
                if not before:
                    query(1, 1)
                    pe.wait_ge(q_float, 4)
                if not more:
                    pe.wait_ge(norm_ready, 5)
                    turn(7, x3, 0)
                now(0)
                next_group(2)
                now(1)
                next_pair(2)
                scores_t(b, s, 4, 0)
                now(2)
                scores_t(b, s, 4, 1)
                next_pair(4)
                now(3)
                next_group(3)
                now(4)
                next_pair(6)
                scores_t(b, s, 5, 0)
                now(5)
                next_group(4)
                now(6)
                now(7)
                if more:
                    turn_max(b + 1, 0)
                scores_t(b, s, 5, 1)

            attend(0, 0, False, True, 16)
            with pe.Fori(0, 3) as i:
                for s in (1, 0):
                    b = 2 * i + 1 if s else 2 * i + 2
                    attend(b, s, True, True, 16 * (i + 2))
            attend(7, 1, True, False, None)
            pe.wait_ge(norm_ready, 6)
            pe.wait_ge(turned_out, 8)
            turn(8, x3, 1, range(BH - 1))

            def gates(h):
                for b in range(h * BH, (h + 1) * BH):
                    for k in range(KB):
                        ins = mm(bank[0:S, 4, b * 2 * E:(b + 1) * 2 * E], x3T[:, k, seq(b)], wrt[:, k, :],
                                 start=k == 0, stop=k == KB - 1)
                if h:
                    ins.then_inc(lg_done, 1)

            def gate_up(e, n, j, halves=(0, 1)):
                f = 8 * e + n
                if halves[0] == 0:
                    if j == 0:
                        at(pe, w_lo, f + 1)
                        at(pe, silu_ready, f)
                    else:
                        at(pe, h_float, f)
                wh, wl = chunk(whi, n % RING, j), chunk(wlo, n % RING, j)
                ins = three_passes([bank[:, 2 * j + h, 0:HALF] for h in halves],
                                   [[(wh[:, k, :], wl[:, k, :], x3hi[:, k, half(h)], x3lo[:, k, half(h)])
                                     for k in range(KB)] for h in halves])
                if halves[-1] == 1:
                    ins.then_inc((g_done, u_done)[j], 1)

            def expert_down(e, n, first=False):
                at(pe, h_split, 8 * e + n + 1)
                if n == 0:
                    at(pe, y_out, KB * e)
                wh, wl = chunk(whi, n % RING, 2), chunk(wlo, n % RING, 2)
                for m in range(KB):
                    if first and m == 1:
                        pe.wait_ge(cwT_ready, 1)
                    ms = slice(m * P, (m + 1) * P)
                    for h in range(2):
                        for i, (w, a) in enumerate(((wh, hhi), (wh, hlo), (wl, hhi))):
                            ins = mm(bank[:, 4 + 2 * m + h, 0:HALF], w[:, ms], a[:, n % 2, half(h)],
                                     start=n == 0 and i == 0, stop=n == NF - 1 and i == 2)
                ins.then_inc(chunk_used, 1)

            def last_down():
                n = NF - 1
                at(pe, h_split, 8 * E)
                wh, wl = chunk(whi, n % RING, 2), chunk(wlo, n % RING, 2)
                for h in range(2):
                    for m in range(KB):
                        ms = slice(m * P, (m + 1) * P)
                        for i, (w, a) in enumerate(((wh, hhi), (wh, hlo), (wl, hhi))):
                            ins = mm(bank[:, 4 + 2 * m + h, 0:HALF], w[:, ms], a[:, n % 2, half(h)],
                                     start=False, stop=i == 2)
                    ins.then_inc(last_done, 1)

            def expert(e):
                for n in range(NF):
                    gate_up(e, n, 0)
                    gate_up(e, n, 1)
                    if n:
                        expert_down(e, n - 1)
                    else:
                        expert_down(e - 1, NF - 1)

            pe.wait_ge(x3_split, 1)
            gate_up(0, 0, 0, (0,))
            weighted(7, 1, 1, range(0, 4))
            gate_up(0, 0, 1, (0,))
            weighted(7, 1, 1, range(4, HH))
            pe.wait_ge(in_router, 16)
            gates(0)
            pe.wait_ge(norm_ready, 7)
            turn(8, x3, 1, range(BH - 1, BH))
            pe.wait_ge(turned_out, 9)
            pe.wait_ge(x3_split, 2)
            gate_up(0, 0, 0, (1,))
            gate_up(0, 0, 1, (1,))
            gates(1)
            for n in range(1, NF):
                gate_up(0, n, 0)
                gate_up(0, n, 1)
                if n == 1:
                    pe.wait_ge(cw_ready, 1)
                    for b in range(B):
                        ins = pe.transpose(bank[0:E, 6 + b // BH, (b % BH) * S:(b % BH + 1) * S],
                                           cw[:, b, :], ident[0:S, 0:S])
                    ins.then_inc(cwT_done, 1)
                expert_down(0, n - 1, n == 1)
            with pe.Fori(1, E) as e:
                expert(e)
            last_down()
            for n in range(4):
                for m in range(KB):
                    pe.wait_ge((last_added0, last_added1)[m], n // 2 + 1)
                    for b in range(2):
                        ins = pe.transpose(bank[0:S, n, b * D + m * P:b * D + (m + 1) * P],
                                           acc[:, m, seq(2 * n + b)], ident)
                ins.then_inc(fin_done, 1)


def kernel(**inputs):
    import numpy as np
    import concourse.bacc as bacc
    from concourse.bass_utils import run_bass_kernel_spmd

    def get(name):
        return np.asarray(inputs[name])

    def block1(name):
        return get("L0_attn_" + name)

    def in_blocks(w):
        return w.reshape(-1, P, w.shape[1]).transpose(1, 0, 2)

    square = np.stack([in_blocks(w.T) for w in (
        block1("Wa_w"), block1("Wb_w"), block1("Wo_w"), block1("C_w"), block1("p_w"),
        get("L0_xattn_Wq"), get("L0_xattn_Wk"), get("L0_xattn_Wv"))], axis=1)
    columns = np.concatenate([v.reshape(-1, P).T for v in (
        block1("Wa_b"), block1("Wb_b"), get("L0_xattn_bq"), get("L0_xattn_bk"), block1("f1_b"), block1("f2_b"))], axis=1)
    rows = np.stack([block1("C_b"), block1("Wo_b"), np.repeat(block1("head_weights"), DH), block1("ln_g"),
                     block1("ln_b"), block1("p_b"), get("L0_xattn_bv")])
    heads = np.arange(P)[:, None] // DH % HG == np.arange(HG)[None, :]
    maxima = (np.arange(P)[:, None] < S) | (np.arange(P)[:, None] - S == np.arange(HH)[None, :])
    arrays = {
        "x": get("x").transpose(1, 0, 2),
        "context": get("ctx_1024").transpose(0, 2, 1).reshape(B, KB, P, SK).transpose(0, 2, 1, 3),
        "mask": get("mask_Bx1xSxS2_ik1").reshape(B, S, SK),
        "square": square,
        "ff1": in_blocks(block1("f1_w").T),
        "ff2": in_blocks(block1("f2_w").T),
        "columns": columns,
        "rows": rows,
        "router": np.concatenate([in_blocks(get("L0_ffn_w_router")), in_blocks(get("L0_ffn_w_gating"))], axis=2),
        "gate": get("L0_ffn_w_gate"),
        "up": get("L0_ffn_w_up"),
        "down": get("L0_ffn_w_down"),
        "constants": np.concatenate([np.eye(P), heads, maxima], axis=1).astype(np.float32),
    }
    arrays = {n: np.ascontiguousarray(a) for n, a in arrays.items()}
    nc = bacc.Bacc("TRN2", target_bir_lowering=False, num_devices=1)
    args = [nc.dram_tensor(n, a.shape, mybir.dt.from_np(a.dtype), kind="ExternalInput").ap() for n, a in arrays.items()]
    y = nc.dram_tensor("y", (B, S, D), F32, kind="ExternalOutput").ap()
    decoder_layer(nc, *args, y)
    got = run_bass_kernel_spmd(nc, [arrays], core_ids=[0])
    return got.results[0]["y"]
```
